# Optimizing a Trainium2 kernel written in Bass

```python
import numpy as np
import jax
import jax.numpy as jnp

def _softmax(x, axis=-1):
    return jax.nn.softmax(x, axis=axis)

def _gelu(x):
    return jax.nn.gelu(x, approximate=True)

def _silu(x):
    return jax.nn.silu(x)

def _sigmoid(x):
    return jax.nn.sigmoid(x)

def _layernorm(x, axis=-1, eps=1e-05):
    m = jnp.mean(x, axis=axis, keepdims=True)
    v = jnp.var(x, axis=axis, keepdims=True)
    return (x - m) / jnp.sqrt(v + eps)

def _scatter_add(tgt, idx, src, axis=0):
    return tgt.at[idx].add(src)

def _segment_sum(src, seg, n):
    return jax.ops.segment_sum(src, seg, n)
kernel_name = 'mk_adaln_d1_jaxref_r4_645181'

def setup_inputs(seed: int=0):
    np.random.seed(seed)
    _w = jnp.asarray

    def _L0_attn_setup():
        import jax, jax.numpy as jnp
        import numpy as np
        DT_MAX = 10.0
        RATE_EPS = 0.0001

        def _ssm_forward(x, W_in, W_state, W_dt, b_dt, A_log, W_C, D, W_out):
            B, L, d_model = x.shape
            ug = jnp.einsum('bld,ed->ble', x, W_in)
            u, gate = jnp.split(ug, 2, axis=-1)
            b_t = jnp.einsum('bld,nd->bln', u, W_state)
            dt_t = jnp.minimum(jax.nn.softplus(jnp.einsum('bld,nd->bln', u, W_dt) + b_dt), DT_MAX)
            rate = jax.nn.softplus(A_log) + RATE_EPS
            decay = jnp.clip(jnp.exp(-dt_t * rate), 0.0, 1.0)

            def step(h, inp):
                d_t, bt = inp
                h = d_t * h + (1.0 - d_t) * bt
                return (h, h)
            h0 = jnp.zeros((B, b_t.shape[-1]), x.dtype)
            xs = (jnp.swapaxes(decay, 0, 1), jnp.swapaxes(b_t, 0, 1))
            _, hs = jax.lax.scan(step, h0, xs)
            hs = jnp.swapaxes(hs, 0, 1)
            y = jnp.einsum('bln,dn->bld', hs, W_C)
            z = y * jax.nn.silu(gate) + x * D
            return jnp.einsum('bld,ed->ble', z, W_out)
        key = jax.random.key(seed)
        ks = jax.random.split(key, 8)
        B, L, D_MODEL, D_STATE = (4, 512, 256, 128)
        s = lambda fan_in: 1.0 / np.sqrt(fan_in)
        return {'x': jax.random.normal(ks[0], (B, L, D_MODEL), jnp.float32), 'W_in': jax.random.normal(ks[1], (2 * D_MODEL, D_MODEL), jnp.float32) * s(D_MODEL), 'W_state': jax.random.normal(ks[2], (D_STATE, D_MODEL), jnp.float32) * s(D_MODEL), 'W_dt': jax.random.normal(ks[3], (D_STATE, D_MODEL), jnp.float32) * s(D_MODEL), 'b_dt': jax.random.normal(ks[4], (D_STATE,), jnp.float32) * s(D_MODEL), 'A_log': jnp.zeros((D_STATE,), jnp.float32), 'W_C': jax.random.normal(ks[5], (D_MODEL, D_STATE), jnp.float32) * s(D_STATE), 'D': jnp.ones((D_MODEL,), jnp.float32), 'W_out': jax.random.normal(ks[6], (D_MODEL, D_MODEL), jnp.float32) * s(D_MODEL)}
    _L0_attn_in = _L0_attn_setup()

    def _L0_ffn_setup():
        import jax, jax.numpy as jnp
        import numpy as np
        DIM = 256

        def _reference_tuple_inner(x, W_r, W_k, W_v, mu_r, mu_k):
            B, T, C = x.shape
            x_prev = jnp.concatenate([jnp.zeros((B, 1, C), x.dtype), x[:, :-1, :]], axis=1)
            xr = mu_r * x + (1.0 - mu_r) * x_prev
            xk = mu_k * x + (1.0 - mu_k) * x_prev
            r = jax.nn.sigmoid(jnp.einsum('btc,dc->btd', xr, W_r))
            k = jnp.einsum('btc,dc->btd', xk, W_k)
            k_act = jnp.square(jax.nn.relu(k))
            out = r * jnp.einsum('btc,dc->btd', k_act, W_v)
            new_state = x[:, -1, :]
            return (out, new_state)
        key = jax.random.key(seed)
        ks = jax.random.split(key, 6)
        B, T, C = (8, 512, DIM)
        x = jax.random.normal(ks[0], (B, T, C), dtype=jnp.float32)
        s = 1.0 / np.sqrt(C)
        W_r = jax.random.uniform(ks[1], (C, C), jnp.float32, -s, s)
        W_k = jax.random.uniform(ks[2], (C, C), jnp.float32, -s, s)
        W_v = jax.random.uniform(ks[3], (C, C), jnp.float32, -s, s)
        mu_r = jax.random.uniform(ks[4], (C,), jnp.float32)
        mu_k = jax.random.uniform(ks[5], (C,), jnp.float32)
        return {'x': x, 'W_r': W_r, 'W_k': W_k, 'W_v': W_v, 'mu_r': mu_r, 'mu_k': mu_k}
    _L0_ffn_in = _L0_ffn_setup()
    _L0_c = _w((lambda *s: np.random.randn(*s).astype(np.float32) * 0.05)(16, 256))
    _L0_wmod = _w((lambda *s: np.random.randn(*s).astype(np.float32) * 0.05)(256, 6 * 256) * 256 ** (-0.5))
    _d = {'L0_attn_x': _L0_attn_in['x'], 'L0_attn_W_in': _L0_attn_in['W_in'], 'L0_attn_W_state': _L0_attn_in['W_state'], 'L0_attn_W_dt': _L0_attn_in['W_dt'], 'L0_attn_b_dt': _L0_attn_in['b_dt'], 'L0_attn_A_log': _L0_attn_in['A_log'], 'L0_attn_W_C': _L0_attn_in['W_C'], 'L0_attn_D': _L0_attn_in['D'], 'L0_attn_W_out': _L0_attn_in['W_out'], 'L0_ffn_W_r': _L0_ffn_in['W_r'], 'L0_ffn_W_k': _L0_ffn_in['W_k'], 'L0_ffn_W_v': _L0_ffn_in['W_v'], 'L0_ffn_mu_r': _L0_ffn_in['mu_r'], 'L0_ffn_mu_k': _L0_ffn_in['mu_k'], 'L0_c': _L0_c, 'L0_wmod': _L0_wmod}
    _x0 = _d['L0_attn_x']
    _d['L0_attn_x'] = jax.random.normal(jax.random.fold_in(jax.random.key(seed), 1), (16, 512, 256), dtype=_x0.dtype)
    del _x0
    return _d

def reference(L0_attn_x, L0_attn_W_in, L0_attn_W_state, L0_attn_W_dt, L0_attn_b_dt, L0_attn_A_log, L0_attn_W_C, L0_attn_D, L0_attn_W_out, L0_ffn_W_r, L0_ffn_W_k, L0_ffn_W_v, L0_ffn_mu_r, L0_ffn_mu_k, L0_c, L0_wmod):

    def _L0_attn_ref(x, W_in, W_state, W_dt, b_dt, A_log, W_C, D, W_out):
        import jax, jax.numpy as jnp
        import numpy as np
        DT_MAX = 10.0
        RATE_EPS = 0.0001

        def _ssm_forward(x, W_in, W_state, W_dt, b_dt, A_log, W_C, D, W_out):
            B, L, d_model = x.shape
            ug = jnp.einsum('bld,ed->ble', x, W_in)
            u, gate = jnp.split(ug, 2, axis=-1)
            b_t = jnp.einsum('bld,nd->bln', u, W_state)
            dt_t = jnp.minimum(jax.nn.softplus(jnp.einsum('bld,nd->bln', u, W_dt) + b_dt), DT_MAX)
            rate = jax.nn.softplus(A_log) + RATE_EPS
            decay = jnp.clip(jnp.exp(-dt_t * rate), 0.0, 1.0)

            def step(h, inp):
                d_t, bt = inp
                h = d_t * h + (1.0 - d_t) * bt
                return (h, h)
            h0 = jnp.zeros((B, b_t.shape[-1]), x.dtype)
            xs = (jnp.swapaxes(decay, 0, 1), jnp.swapaxes(b_t, 0, 1))
            _, hs = jax.lax.scan(step, h0, xs)
            hs = jnp.swapaxes(hs, 0, 1)
            y = jnp.einsum('bln,dn->bld', hs, W_C)
            z = y * jax.nn.silu(gate) + x * D
            return jnp.einsum('bld,ed->ble', z, W_out)
        return _ssm_forward(x, W_in, W_state, W_dt, b_dt, A_log, W_C, D, W_out)

    def _L0_ffn_ref(x, W_r, W_k, W_v, mu_r, mu_k):
        import jax, jax.numpy as jnp
        import numpy as np
        DIM = 256

        def _reference_tuple_inner(x, W_r, W_k, W_v, mu_r, mu_k):
            B, T, C = x.shape
            x_prev = jnp.concatenate([jnp.zeros((B, 1, C), x.dtype), x[:, :-1, :]], axis=1)
            xr = mu_r * x + (1.0 - mu_r) * x_prev
            xk = mu_k * x + (1.0 - mu_k) * x_prev
            r = jax.nn.sigmoid(jnp.einsum('btc,dc->btd', xr, W_r))
            k = jnp.einsum('btc,dc->btd', xk, W_k)
            k_act = jnp.square(jax.nn.relu(k))
            out = r * jnp.einsum('btc,dc->btd', k_act, W_v)
            new_state = x[:, -1, :]
            return (out, new_state)
        return _reference_tuple_inner(x, W_r, W_k, W_v, mu_r, mu_k)[0]
    x = L0_attn_x
    mod = (_silu(L0_c) @ L0_wmod).reshape(L0_c.shape[0], 6, 1, -1)
    sa, ca, ga, sb, cb, gb = (mod[:, 0], mod[:, 1], mod[:, 2], mod[:, 3], mod[:, 4], mod[:, 5])
    ga = (2 * (ga >= 0) - 1) * jnp.maximum(jnp.abs(ga), 0.25)
    gb = (2 * (gb >= 0) - 1) * jnp.maximum(jnp.abs(gb), 0.25)
    h = _layernorm(x, axis=-1) * (1 + ca) + sa
    x = x + ga * _L0_attn_ref(h, L0_attn_W_in, L0_attn_W_state, L0_attn_W_dt, L0_attn_b_dt, L0_attn_A_log, L0_attn_W_C, L0_attn_D, L0_attn_W_out)
    h = _layernorm(x, axis=-1) * (1 + cb) + sb
    x = x + gb * _L0_ffn_ref(h, L0_ffn_W_r, L0_ffn_W_k, L0_ffn_W_v, L0_ffn_mu_r, L0_ffn_mu_k)
    return x

_drawn_inputs = setup_inputs


def setup_inputs(seed=0):
    import zlib

    import numpy as np

    out = dict(_drawn_inputs(seed))
    spreads = {'L0_attn_A_log': (0.0, 0.8), 'L0_attn_D': (1.0, 0.2)}
    factors = {'L0_attn_b_dt': 8.0,
     'L0_ffn_W_r': 8.0,
     'L0_ffn_W_k': 3.13,
     'L0_ffn_W_v': 2.869,
     'L0_ffn_mu_r': 8.0,
     'L0_ffn_mu_k': 5.186}
    for name, (base, spread) in spreads.items():
        noise = np.random.default_rng([zlib.crc32(name.encode()), seed]).standard_normal(out[name].shape)
        drawn = base * np.exp(spread * noise) if base else spread * noise
        out[name] = jnp.asarray(drawn.astype(out[name].dtype))
    for name, factor in factors.items():
        out[name] = (out[name] * factor).astype(out[name].dtype)
    return out
```

```python
from contextlib import ExitStack

import numpy as np

import concourse.bass as bass
from concourse import mybir

F32 = mybir.dt.float32
F32R = mybir.dt.float32r
ALU = mybir.AluOpType
ACT = mybir.ActivationFunctionType

P = 128
EPS = 1e-5
RATE_EPS = 1e-4
DT_MAX = 10.0
GATE_MIN = 0.25


def before(eng, sem, count):
    if not isinstance(count, int) or count > 0:
        eng.wait_ge(sem, count)


def adaln_block(nc, x_tok_d, x_ch_d, w_d, wmod_d, c_d, cols_d, ident_d, out_d):
    NB, T, C = x_tok_d.shape
    CH = C // P
    TT = T // P
    NS = P
    EXP_MAX = float(np.expm1(DT_MAX))

    with ExitStack() as ctx:
        def sb(name, shape, dt=F32):
            return ctx.enter_context(nc.sbuf_tensor(name, shape, dt))

        def sem(name):
            return ctx.enter_context(nc.semaphore(name))

        w_raw = sb("w_raw", [P, w_d.shape[1]])
        names = [("in_u", C), ("dt_state", 2 * NS), ("gate", C), ("out", C), ("r", C), ("k", C), ("v", C), ("y", C // 2)]
        raw, at = {}, 0
        for name, n in names:
            raw[name] = w_raw[:, at:at + CH * n].rearrange("p (c n) -> p c n", c=CH)
            at += CH * n
        w_y = w_raw[:, at - C:at]
        wmod = sb("wmod", [P, CH, 6 * C])
        w_front = sb("w_front", [P, CH, 2 * NS])
        wf_hi = sb("wf_hi", [P, CH, 2 * NS + C], F32R)
        wf_lo = sb("wf_lo", [P, CH, 2 * NS + C], F32R)
        ident = sb("ident", [P, P])
        cols = sb("cols", [P, 8])
        c_sb = sb("c_sb", [P, CH * NB])
        c_silu = sb("c_silu", [P, CH * NB])
        mod = sb("mod", [P, 12, NB])
        gate_abs = sb("gate_abs", [P, CH, NB])
        gate_sgn = sb("gate_sgn", [P, CH, NB])
        rate = sb("rate", [P, 3])
        half_neg = sb("half_neg", [P, TT])
        eps = sb("eps", [P, TT])
        B_DT, A_LOG, D0, MU_R, MU_K = 0, 1, 2, 4, 6

        x_tok = sb("x_tok", [P, 2, TT, C])
        x_ch = sb("x_ch", [P, 2, CH, T])
        x1 = sb("x1", [P, 2, CH, T])
        stats1 = sb("stats1", [P, TT, 6])
        mv1 = sb("mv1", [P, 5, TT])
        rstd1 = sb("rstd1", [P, TT])
        xn1 = sb("xn1", [P, TT, C])
        stats2 = sb("stats2", [P, TT, 6])
        mv2 = sb("mv2", [P, 5, TT])
        rstd2 = sb("rstd2", [P, TT])
        xn2 = sb("xn2", [P, TT, C])
        h = sb("h", [P, 2, CH, T])
        h_hi = sb("h_hi", [P, CH, T], F32R)
        h_lo = sb("h_lo", [P, CH, T], F32R)
        dt_e = sb("dt_e", [P, T])
        dt_l = sb("dt_l", [P, T])
        decay = sb("decay", [P, T])
        drive = sb("drive", [P, T])
        state = sb("state", [P, T])
        silu = sb("silu", [P, CH, T])
        yg = sb("yg", [P, CH, T])
        z = sb("z", [P, CH, T])
        h2 = sb("h2", [P, CH, T + 1])
        h2_diff = sb("h2_diff", [P, CH, T])
        xr = sb("xr", [P, CH, T])
        xk = sb("xk", [P, CH, T])
        k_relu = sb("k_relu", [P, CH, T])
        k_act = sb("k_act", [P, CH, T])
        r_tanh = sb("r_tanh", [P, CH, T])
        r_gate = sb("r_gate", [P, 2, CH, T])
        rv = sb("rv", [P, CH, T])

        slot = [ctx.enter_context(nc.psum_tensor(f"slot{i}", [P, CH, T], F32)) for i in range(4)]
        ps_front, ps_y = slot[0], slot[0]
        ps_gate, ps_o = slot[1], slot[1]
        ps_h2, ps_k = slot[2], slot[2]
        ps_x1 = slot[2][:].rearrange("p a b -> p (a b)").rearrange("p (t c) -> p t c", t=TT)
        ps_v, ps_h, ps_r = slot[3], slot[3], slot[3]

        s_w, s_wmod, s_cols, s_c, s_id = sem("w_in"), sem("wmod_in"), sem("cols_in"), sem("c_in"), sem("ident_in")
        s_xt = [sem("x_tok_in0"), sem("x_tok_in1")]
        s_xc = [sem("x_ch_in0"), sem("x_ch_in1")]
        s_out = [sem("x2_out0"), sem("x2_out1")]
        csilu_ok, mod_ps, mod_ok, front_ps, front_ok = sem("csilu_ok"), sem("mod_ps"), sem("mod_ok"), sem("front_ps"), sem("front_ok")
        mod_step, rate_step, rate_exp, rate_ln, rate_ok = sem("mod_step"), sem("rate_step"), sem("rate_exp"), sem("rate_ln"), sem("rate_ok")
        wsplit_hi, wsplit_lo, consts_ok = sem("wsplit_hi"), sem("wsplit_lo"), sem("consts_ok")
        t1_ps, dt_ps, b_ps, g_ps, y_ps, o_ps = sem("t1_ps"), sem("dt_ps"), sem("b_ps"), sem("g_ps"), sem("y_ps"), sem("o_ps")
        t2_ps, t3_ps, k_ps, r_ps, v_ps = sem("t2_ps"), sem("t3_ps"), sem("k_ps"), sem("r_ps"), sem("v_ps")
        h_ok, hhi_ok, e_ok, l_ok, decay_ok, h2_ok = sem("h_ok"), sem("hhi_ok"), sem("e_ok"), sem("l_ok"), sem("decay_ok"), sem("h2_ok")
        silu_ok, relu_ok, tanh_ok, rgate_ok = sem("silu_ok"), sem("relu_ok"), sem("tanh_ok"), sem("rgate_ok")
        st1_ok, mv1_ok, xn1_ok, st2_ok, mv2_ok, xn2_ok = sem("st1_ok"), sem("mv1_ok"), sem("xn1_ok"), sem("st2_ok"), sem("mv2_ok"), sem("xn2_ok")
        halves1_ok, spread1_ok, halves2_ok, spread2_ok = sem("halves1_ok"), sem("spread1_ok"), sem("halves2_ok"), sem("spread2_ok")
        clip_ok, drive_ok, state_ok, yg_ok, z_ok, x1_ok = sem("clip_ok"), sem("drive_ok"), sem("state_ok"), sem("yg_ok"), sem("z_ok"), sem("x1_ok")
        xk_ok, xr_ok, rv_ok = sem("xk_ok"), sem("xr_ok"), sem("rv_ok")
        hlo_ok, diff_ok, kact_ok, x2_ok = sem("hlo_ok"), sem("diff_ok"), sem("kact_ok"), sem("x2_ok")
        var1_ok, rstd1_ok, var2_ok, rstd2_ok = sem("var1_ok"), sem("rstd1_ok"), sem("var2_ok"), sem("rstd2_ok")

        def col(j):
            return cols[:, j:j + 1]

        def mod_at(j, k):
            return mod[:, j, bass.ds(k, 1)]

        def number(m, r):
            return 2 * m + r

        def turn(m, r):
            return m + r // 2 + 1

        def schedule(eng, iteration):
            for k in range(3):
                iteration(0, k)
            with eng.Fori(1, NB // 2 - 1) as m:
                for r in (1, 2):
                    iteration(m, r)
            for k in range(NB - 1, NB + 2):
                iteration(0, k)

        def runs(m, r, first, last):
            return not isinstance(m, int) or first <= 2 * m + r <= last

        block = ctx.enter_context(nc.Block())

        @block.sync
        def _(sp):
            sp.dma_start(c_sb[:], c_d).then_inc(s_c, 16)
            sp.dma_start(x_tok[:, 0], x_tok_d[0].rearrange("(t p) c -> p t c", p=P)).then_inc(s_xt[0], 16)
            sp.dma_start(cols[:], cols_d).then_inc(s_cols, 16)
            sp.dma_start(ident[:], ident_d).then_inc(s_id, 16)
            sp.dma_start(w_raw[:], w_d).then_inc(s_w, 16)
            sp.dma_start(wmod[:], wmod_d.rearrange("(c p) n -> p c n", p=P)).then_inc(s_wmod, 16)
            sp.dma_start(x_ch[:, 0], x_ch_d[0].rearrange("(c p) t -> p c t", p=P)).then_inc(s_xc[0], 16)

            def iteration(m, r):
                k = number(m, r)
                if runs(m, r, 0, NB - 2):
                    q = (r + 1) % 2
                    before(sp, xn1_ok, k)
                    sp.dma_start(x_tok[:, q], x_tok_d[bass.ds(k + 1, 1)].rearrange("b (t p) c -> p (b t) c", p=P)).then_inc(s_xt[q], 16)
                    before(sp, x1_ok, k)
                    sp.dma_start(x_ch[:, q], x_ch_d[bass.ds(k + 1, 1)].rearrange("b (c p) t -> p (b c) t", p=P)).then_inc(s_xc[q], 16)
                if runs(m, r, 2, NB + 1):
                    before(sp, x2_ok, k - 1)
                    sp.dma_start(out_d[bass.ds(k - 2, 1)].rearrange("b (c p) t -> p (b c) t", p=P), x1[:, r % 2]).then_inc(s_out[r % 2], 16)

            schedule(sp, iteration)
            for q in range(2):
                sp.wait_ge(s_out[q], 16 * (NB // 2))

        @block.tensor
        def _(pe):
            def product(out, w, half, m_lo, x, wx=None):
                for c in half:
                    last = nc.tensor.matmul(out, w[:, c, m_lo:m_lo + P], x[:, c, 0:T], start=(c == half[0]), stop=(c == half[-1]))
                return last

            def split_product(out, m_lo):
                parts = [(w, xx, c) for w, xx in ((wf_hi, h_hi), (wf_lo, h_hi), (wf_hi, h_lo)) for c in range(CH)]
                for n, (w, xx, c) in enumerate(parts):
                    last = nc.tensor.matmul(out, w[:, c, m_lo:m_lo + P], xx[:, c, :], start=(n == 0), stop=(n == len(parts) - 1))
                return last

            pe.wait_ge(s_wmod, 16)
            pe.wait_ge(csilu_ok, 1)
            for j in range(12):
                for c in range(CH):
                    last = nc.tensor.matmul(slot[0][:, 0, j * NB:(j + 1) * NB], wmod[:, c, j * P:(j + 1) * P],
                                            c_silu[:, c * NB:(c + 1) * NB], start=(c == 0), stop=(c == CH - 1))
            last.then_inc(mod_ps, 1)
            pe.wait_ge(s_w, 16)
            for a in range(CH):
                for c in range(CH):
                    last = nc.tensor.matmul(slot[1][:, a, 0:2 * NS], raw["in_u"][:, c, a * P:(a + 1) * P], raw["dt_state"][:, c, :],
                                            start=(c == 0), stop=(c == CH - 1))
            last.then_inc(front_ps, 1)
            pe.wait_ge(s_id, 16)

            def t1(k):
                before(pe, xn1_ok, k + 1)
                before(pe, rv_ok, k - 2)
                if isinstance(k, int) and k == 0:
                    pass
                for c in range(CH):
                    for t in range(TT):
                        last = nc.tensor.transpose(ps_h[:, c, t * P:(t + 1) * P], xn1[:, t, c * P:(c + 1) * P], ident[:])
                last.then_inc(t1_ps, 1)

            t1(0)

            def iteration(m, r):
                k = number(m, r)
                if runs(m, r, 0, NB - 1):
                    if isinstance(k, int) and k == 0:
                        pe.wait_ge(wsplit_lo, 2)
                        pe.wait_ge(mod_ok, 1)
                    before(pe, hhi_ok, k + 1)
                    before(pe, hlo_ok, k + 1)
                    before(pe, yg_ok, k)
                    split_product(ps_front[:, 0, :], 0).then_inc(dt_ps, 1)
                    split_product(ps_front[:, 1, :], NS).then_inc(b_ps, 1)
                    before(pe, x1_ok, k)
                    for g in range(CH):
                        last = split_product(ps_gate[:, g, :], 2 * NS + g * P)
                    last.then_inc(g_ps, 1)
                if runs(m, r, 1, NB):
                    before(pe, xn2_ok, k)
                    for c in range(CH):
                        for t in range(TT):
                            last = nc.tensor.transpose(ps_h2[:, c, t * P:(t + 1) * P], xn2[:, t, c * P:(c + 1) * P], ident[:])
                    last.then_inc(t3_ps, 1)
                if runs(m, r, 2, NB + 1):
                    before(pe, kact_ok, k - 1)
                    before(pe, tanh_ok, k - 1)
                    for d in range(CH):
                        last = product(ps_v[:, d, :], raw["v"], range(CH), d * P, k_act)
                    last.then_inc(v_ps, 1)
                if runs(m, r, 0, NB - 1):
                    before(pe, state_ok, k + 1)
                    for d in range(CH):
                        last = nc.tensor.matmul(ps_y[:, d, :], w_y[:, d * P:(d + 1) * P], state[:], start=True, stop=True)
                    last.then_inc(y_ps, 1)
                if runs(m, r, 1, NB):
                    before(pe, xk_ok, k)
                    for d in range(CH):
                        last = product(ps_k[:, d, :], raw["k"], range(CH), d * P, xk)
                    last.then_inc(k_ps, 1)
                if runs(m, r, 0, NB - 2):
                    before(pe, xn1_ok, k + 2)
                    before(pe, rv_ok, k - 1)
                    if isinstance(k, int) and 1 <= k:
                        pass
                    before(pe, hhi_ok, k + 1)
                    for c in range(CH):
                        for t in range(TT):
                            last = nc.tensor.transpose(ps_h[:, c, t * P:(t + 1) * P], xn1[:, t, c * P:(c + 1) * P], ident[:])
                    last.then_inc(t1_ps, 1)
                if runs(m, r, 0, NB - 1):
                    before(pe, z_ok, k + 1)
                    before(pe, silu_ok, k + 1)
                    for d in range(CH):
                        last = product(ps_o[:, d, :], raw["out"], range(CH), d * P, z)
                    last.then_inc(o_ps, 1)
                if runs(m, r, 1, NB):
                    before(pe, xr_ok, k)
                    if runs(m, r, 1, NB - 2):
                        before(pe, hhi_ok, k + 2)
                    before(pe, rv_ok, k - 1)
                    for d in range(CH):
                        last = product(ps_r[:, d, :], raw["r"], range(CH), d * P, xr)
                    last.then_inc(r_ps, 1)
                if runs(m, r, 0, NB - 1):
                    before(pe, x1_ok, k + 1)
                    before(pe, relu_ok, k)
                    for t in range(TT):
                        for c in range(CH):
                            last = nc.tensor.transpose(ps_x1[:, t, c * P:(c + 1) * P], x1[:, r % 2, c, t * P:(t + 1) * P], ident[:])
                    last.then_inc(t2_ps, 1)

            schedule(pe, iteration)

        @block.scalar
        def _(act):
            act.wait_ge(s_c, 16)
            nc.scalar.activation(c_silu[:], c_sb[:], ACT.Silu).then_inc(csilu_ok, 1)
            act.wait_ge(rate_step, 2)
            nc.scalar.activation(rate[:, 1:2], rate[:, 0:1], ACT.Exp, scale=-1.0).then_inc(rate_exp, 1)
            act.wait_ge(rate_exp, 1)
            nc.scalar.activation(rate[:, 2:3], rate[:, 1:2], ACT.Ln, bias=1.0).then_inc(rate_ln, 1)

            def h_evac(k, q):
                before(act, t1_ps, k + 1)
                before(act, z_ok, k - 1)
                before(act, g_ps, k)
                for c in range(CH):
                    last = nc.scalar.activation(h[:, q, c, :], ps_h[:, c, :], ACT.Identity, bias=mod_at(c, k), scale=mod_at(2 + c, k))
                last.then_inc(h_ok, 1)
                for c in range(CH):
                    last = nc.scalar.activation(h_hi[:, c, :], ps_h[:, c, :], ACT.Identity, bias=mod_at(c, k), scale=mod_at(2 + c, k))
                last.then_inc(hhi_ok, 1)

            act.wait_ge(mod_ok, 1)
            act.wait_ge(rate_ok, 1)
            h_evac(0, 0)

            def iteration(m, r):
                k = number(m, r)
                if runs(m, r, 0, NB - 1):
                    before(act, dt_ps, k + 1)
                    nc.scalar.activation(dt_e[:], ps_front[:, 0, :], ACT.Exp, bias=col(B_DT)).then_inc(e_ok, 1)
                    before(act, clip_ok, k + 1)
                    nc.scalar.activation(dt_l[:], dt_e[:], ACT.Ln, bias=1.0).then_inc(l_ok, 1)
                    before(act, l_ok, k + 1)
                    before(act, state_ok, k)
                    nc.scalar.activation(decay[:], dt_l[:], ACT.Exp, scale=rate[:, 0:1]).then_inc(decay_ok, 1)
                    before(act, g_ps, k + 1)
                    before(act, yg_ok, k)
                    nc.scalar.activation(silu[:], ps_gate[:], ACT.Silu).then_inc(silu_ok, 1)
                if runs(m, r, 1, NB):
                    before(act, t3_ps, k)
                    before(act, xr_ok, k - 1)
                    before(act, diff_ok, k - 1)
                    for c in range(CH):
                        last = nc.scalar.activation(h2[:, c, 1:T + 1], ps_h2[:, c, :], ACT.Identity, bias=mod_at(6 + c, k - 1), scale=mod_at(8 + c, k - 1))
                    last.then_inc(h2_ok, 1)
                    before(act, k_ps, k)
                    before(act, kact_ok, k - 1)
                    nc.scalar.activation(k_relu[:], ps_k[:], ACT.Relu).then_inc(relu_ok, 1)
                if runs(m, r, 0, NB - 2):
                    h_evac(k + 1, (r + 1) % 2)
                if runs(m, r, 1, NB):
                    q = (r + 1) % 2
                    before(act, r_ps, k)
                    nc.scalar.activation(r_tanh[:], ps_r[:], ACT.Tanh, scale=0.5).then_inc(tanh_ok, 1)
                    before(act, tanh_ok, k)
                    before(act, rv_ok, k - 2)
                    for c in range(CH):
                        last = nc.scalar.activation(r_gate[:, q, c, :], r_tanh[:, c, :], ACT.Identity, bias=mod_at(10 + c, k - 1), scale=mod_at(10 + c, k - 1))
                    last.then_inc(rgate_ok, 1)

            schedule(act, iteration)

        @block.vector
        def _(dve):
            steps = [0]

            def chained(sem_, ins, count=None):
                steps[0] += 1
                ins.then_inc(sem_, 1)
                dve.wait_ge(sem_, steps[0])

            def stats(x, st, mv, st_ok, halves_ok, spread_ok, mv_ok, k):
                for t in range(TT):
                    last = nc.vector.bn_stats(st[:, t, :], x[:, t, :])
                last.then_inc(st_ok, 1)
                before(dve, st_ok, k + 1)
                nc.vector.tensor_tensor(mv[:, 2, :], st[:, :, 1], st[:, :, 4], ALU.subtract)
                nc.vector.tensor_tensor(mv[:, 3, :], st[:, :, 2], st[:, :, 5], ALU.add).then_inc(halves_ok, 1)
                before(dve, halves_ok, k + 1)
                nc.vector.scalar_tensor_tensor(mv[:, 0, :], mv[:, 2, :], -0.5, st[:, :, 1], ALU.mult, ALU.add)
                nc.vector.scalar_tensor_tensor(mv[:, 4, :], mv[:, 2, :], 0.25, mv[:, 2, :], ALU.mult, ALU.mult).then_inc(spread_ok, 1)
                before(dve, spread_ok, k + 1)
                nc.vector.scalar_tensor_tensor(mv[:, 1, :], mv[:, 3, :], 1.0 / C, mv[:, 4, :], ALU.mult, ALU.add).then_inc(mv_ok, 1)

            def normalise(xn, x, mv, rstd, done):
                for t in range(TT):
                    last = nc.vector.tensor_scalar(xn[:, t, :], x[:, t, :], mv[:, 0, t:t + 1], rstd[:, t:t + 1], ALU.subtract, ALU.mult)
                last.then_inc(done, 1)

            def ln1_stats(k, q, n):
                before(dve, s_xt[q], 16 * n)
                stats(x_tok[:, q], stats1, mv1, st1_ok, halves1_ok, spread1_ok, mv1_ok, k)

            def ln1_apply(k, q):
                before(dve, rstd1_ok, k + 1)
                before(dve, t1_ps, k)
                normalise(xn1, x_tok[:, q], mv1, rstd1, xn1_ok)

            nc.vector.memset(half_neg[:], -0.5)
            nc.vector.memset(eps[:], EPS)
            nc.vector.memset(h2[:, :, 0:1], 0.0).then_inc(consts_ok, 1)
            ln1_stats(0, 0, 1)
            dve.wait_ge(s_cols, 16)
            nc.vector.tensor_scalar(rate[:, 1:2], col(A_LOG), -1.0, None, ALU.mult).then_inc(rate_step, 1)
            dve.wait_ge(rate_step, 1)
            nc.vector.tensor_tensor(rate[:, 0:1], rate[:, 1:2], col(A_LOG), ALU.max).then_inc(rate_step, 1)
            ln1_apply(0, 0)
            dve.wait_ge(front_ps, 1)
            nc.vector.tensor_copy(w_front[:], slot[1][:, :, 0:2 * NS]).then_inc(front_ok, 1)
            dve.wait_ge(front_ok, 1)
            nc.vector.tensor_copy(wf_hi[:, :, 0:2 * NS], w_front[:])
            nc.vector.tensor_copy(wf_hi[:, :, 2 * NS:], raw["gate"]).then_inc(wsplit_hi, 1)
            dve.wait_ge(wsplit_hi, 1)
            nc.vector.tensor_tensor(wf_lo[:, :, 0:2 * NS], w_front[:], wf_hi[:, :, 0:2 * NS].bitcast(F32), ALU.subtract).then_inc(wsplit_lo, 1)
            nc.vector.tensor_tensor(wf_lo[:, :, 2 * NS:], raw["gate"], wf_hi[:, :, 2 * NS:].bitcast(F32), ALU.subtract).then_inc(wsplit_lo, 1)
            dve.wait_ge(mod_ps, 1)
            chained(mod_step, nc.vector.tensor_copy(mod[:], slot[0][:, 0, 0:12 * NB].rearrange("p (j b) -> p j b", b=NB)))
            for j in (2, 8):
                chained(mod_step, nc.vector.tensor_scalar(mod[:, j:j + CH, :], mod[:, j:j + CH, :], 1.0, None, ALU.add))
            for j, scale in ((4, 1.0), (10, 0.5)):
                g = mod[:, j:j + CH, :]
                chained(mod_step, nc.vector.tensor_scalar(gate_abs[:], g, -1.0, None, ALU.mult))
                chained(mod_step, nc.vector.tensor_tensor(gate_abs[:], gate_abs[:], g, ALU.max))
                chained(mod_step, nc.vector.tensor_scalar(gate_abs[:], gate_abs[:], GATE_MIN, scale, ALU.max, ALU.mult))
                chained(mod_step, nc.vector.tensor_scalar(gate_sgn[:], g, 0.0, 2.0, ALU.is_ge, ALU.mult))
                chained(mod_step, nc.vector.tensor_scalar(gate_sgn[:], gate_sgn[:], -1.0, None, ALU.add))
                chained(mod_step, nc.vector.tensor_tensor(g, gate_sgn[:], gate_abs[:], ALU.mult))
            dve.wait_ge(rate_ln, 1)
            nc.vector.tensor_scalar(rate[:, 0:1], col(A_LOG), 0.0, RATE_EPS, ALU.max, ALU.add).then_inc(rate_step, 1)
            dve.wait_ge(rate_step, 3)
            nc.vector.tensor_tensor(rate[:, 0:1], rate[:, 0:1], rate[:, 2:3], ALU.add).then_inc(rate_step, 1)
            dve.wait_ge(rate_step, 4)
            nc.vector.tensor_scalar(rate[:, 0:1], rate[:, 0:1], -1.0, None, ALU.mult).then_inc(rate_ok, 1)
            dve.wait_ge(rate_ok, 1)
            nc.vector.tensor_copy(rate[:, 1:2], rate[:, 0:1]).then_inc(mod_ok, 1)

            def iteration(m, r):
                k = number(m, r)
                p = r % 2
                front, middle, tail = runs(m, r, 0, NB - 1), runs(m, r, 1, NB), runs(m, r, 2, NB + 1)
                if middle:
                    before(dve, t2_ps, k)
                    stats(ps_x1, stats2, mv2, st2_ok, halves2_ok, spread2_ok, mv2_ok, k - 1)
                if front:
                    before(dve, e_ok, k + 1)
                    nc.vector.tensor_scalar(dt_e[:], dt_e[:], EXP_MAX, None, ALU.min).then_inc(clip_ok, 1)
                if middle:
                    before(dve, rstd2_ok, k)
                    normalise(xn2, ps_x1, mv2, rstd2, xn2_ok)
                if front:
                    before(dve, decay_ok, k + 1)
                    before(dve, b_ps, k + 1)
                    nc.vector.scalar_tensor_tensor(drive[:], decay[:], 1.0, ps_front[:, 1, :], ALU.subtract, ALU.mult).then_inc(drive_ok, 1)
                    before(dve, drive_ok, k + 1)
                    before(dve, y_ps, k)
                    nc.vector.tensor_tensor_scan(state[:], decay[:], drive[:], 0.0, ALU.mult, ALU.subtract).then_inc(state_ok, 1)
                if middle:
                    before(dve, diff_ok, k)
                    before(dve, k_ps, k - 1)
                    for c in range(CH):
                        last = nc.vector.scalar_tensor_tensor(xk[:, c, :], h2_diff[:, c, :], col(MU_K + c), h2[:, c, 0:T], ALU.mult, ALU.add)
                    last.then_inc(xk_ok, 1)
                if runs(m, r, 0, NB - 2):
                    ln1_stats(k + 1, (r + 1) % 2, turn(m, r + 1))
                if front:
                    before(dve, y_ps, k + 1)
                    before(dve, silu_ok, k + 1)
                    nc.vector.tensor_tensor(yg[:], silu[:], ps_y[:], ALU.mult).then_inc(yg_ok, 1)
                    before(dve, yg_ok, k + 1)
                    before(dve, o_ps, k)
                    before(dve, h_ok, k + 1)
                    for c in range(CH):
                        last = nc.vector.scalar_tensor_tensor(z[:, c, :], h[:, p, c, :], col(D0 + c), yg[:, c, :], ALU.mult, ALU.add)
                    last.then_inc(z_ok, 1)
                if runs(m, r, 0, NB - 2):
                    ln1_apply(k + 1, (r + 1) % 2)
                if middle:
                    before(dve, r_ps, k - 1)
                    for c in range(CH):
                        last = nc.vector.scalar_tensor_tensor(xr[:, c, :], h2_diff[:, c, :], col(MU_R + c), h2[:, c, 0:T], ALU.mult, ALU.add)
                    last.then_inc(xr_ok, 1)
                if tail:
                    before(dve, v_ps, k - 1)
                    before(dve, rgate_ok, k - 1)
                    before(dve, x2_ok, k - 2)
                    nc.vector.tensor_tensor(rv[:], r_gate[:, p], ps_v[:], ALU.mult).then_inc(rv_ok, 1)
                if front:
                    before(dve, o_ps, k + 1)
                    before(dve, s_xc[p], 16 * turn(m, r))
                    before(dve, s_out[p], 16 * (turn(m, r) - 1))
                    for c in range(CH):
                        last = nc.vector.scalar_tensor_tensor(x1[:, p, c, :], ps_o[:, c, :], mod_at(4 + c, k), x_ch[:, p, c, :], ALU.mult, ALU.add)
                    last.then_inc(x1_ok, 1)

            schedule(dve, iteration)

        @block.gpsimd
        def _(pool):
            def inv_std(mv, rstd, mv_ok, var_ok, rstd_ok, k):
                before(pool, mv_ok, k + 1)
                nc.gpsimd.tensor_tensor(rstd[:], mv[:, 1, :], eps[:], ALU.add).then_inc(var_ok, 1)
                before(pool, var_ok, k + 1)
                nc.gpsimd.tensor_tensor(rstd[:], rstd[:], half_neg[:], ALU.pow).then_inc(rstd_ok, 1)

            def low_part(k, q):
                before(pool, hhi_ok, k + 1)
                before(pool, g_ps, k)
                nc.gpsimd.tensor_tensor(h_lo[:], h[:, q], h_hi[:].bitcast(F32), ALU.subtract).then_inc(hlo_ok, 1)

            pool.wait_ge(consts_ok, 1)
            inv_std(mv1, rstd1, mv1_ok, var1_ok, rstd1_ok, 0)
            low_part(0, 0)

            def iteration(m, r):
                k = number(m, r)
                p = r % 2
                if runs(m, r, 1, NB):
                    inv_std(mv2, rstd2, mv2_ok, var2_ok, rstd2_ok, k - 1)
                    before(pool, h2_ok, k)
                    before(pool, xr_ok, k - 1)
                    nc.gpsimd.tensor_tensor(h2_diff[:], h2[:, :, 1:T + 1], h2[:, :, 0:T], ALU.subtract).then_inc(diff_ok, 1)
                if runs(m, r, 0, NB - 2):
                    inv_std(mv1, rstd1, mv1_ok, var1_ok, rstd1_ok, k + 1)
                if runs(m, r, 1, NB):
                    before(pool, relu_ok, k)
                    before(pool, v_ps, k - 1)
                    nc.gpsimd.tensor_tensor(k_act[:], k_relu[:], k_relu[:], ALU.mult).then_inc(kact_ok, 1)
                if runs(m, r, 0, NB - 2):
                    low_part(k + 1, (r + 1) % 2)
                if runs(m, r, 2, NB + 1):
                    before(pool, rv_ok, k - 1)
                    before(pool, t2_ps, k - 1)
                    nc.gpsimd.tensor_tensor(x1[:, p], x1[:, p], rv[:], ALU.add).then_inc(x2_ok, 1)

            schedule(pool, iteration)


def kernel(**inputs):
    import concourse.bacc as bacc
    from concourse.bass_utils import run_bass_kernel_spmd

    a = {name.replace("L0_", "").replace("attn_", "").replace("ffn_", ""): np.asarray(v) for name, v in inputs.items()}
    C = a["x"].shape[2]

    def halves(w):
        return w.reshape(-1, P, w.shape[1]).transpose(1, 0, 2).reshape(P, -1)

    x = np.ascontiguousarray(a["x"])
    arrays = {
        "x_tok": x,
        "x_ch": np.ascontiguousarray(x.transpose(0, 2, 1)),
        "weights": np.ascontiguousarray(np.concatenate([
            halves(a["W_in"][:C]),
            halves(np.concatenate([a["W_dt"].T, a["W_state"].T], axis=1)),
            halves(a["W_in"][C:].T), halves(a["W_out"].T),
            halves(a["W_r"].T), halves(a["W_k"].T), halves(a["W_v"].T), halves(a["W_C"].T),
        ], axis=1)),
        "wmod": np.ascontiguousarray(a["wmod"]),
        "c": np.ascontiguousarray(halves(a["c"].T)),
        "cols": np.ascontiguousarray(np.stack([a["b_dt"], a["A_log"], *(v.reshape(-1, P)[i] for v in (a["D"], a["mu_r"], a["mu_k"])
                                                                        for i in range(2))], axis=1)),
        "ident": np.eye(P, dtype=np.float32),
    }
    arrays = {f"{name}_in": v for name, v in arrays.items()}
    nc = bacc.Bacc("TRN2", target_bir_lowering=False, num_devices=1)
    aps = [nc.dram_tensor(name, v.shape, F32, kind="ExternalInput").ap() for name, v in arrays.items()]
    out = nc.dram_tensor("x2_out", arrays["x_ch_in"].shape, F32, kind="ExternalOutput").ap()
    adaln_block(nc, *aps, out)
    got = run_bass_kernel_spmd(nc, [arrays], core_ids=[0]).results[0]["x2_out"]
    return np.ascontiguousarray(got.transpose(0, 2, 1))
```

```python
from contextlib import ExitStack

import numpy as np

import concourse.bass as bass
from concourse import mybir

F32 = mybir.dt.float32
F32R = mybir.dt.float32r
ALU = mybir.AluOpType
ACT = mybir.ActivationFunctionType

P = 128
EPS = 1e-5
RATE_EPS = 1e-4
DT_MAX = 10.0
GATE_MIN = 0.25


def before(eng, sem, count):
    if not isinstance(count, int) or count > 0:
        eng.wait_ge(sem, count)


def adaln_block(nc, x_tok_d, x_ch_d, w_d, wmod_d, c_d, cols_d, ident_d, out_d):
    NB, T, C = x_tok_d.shape
    CH = C // P
    TT = T // P
    NS = P
    EXP_MAX = float(np.expm1(DT_MAX))

    with ExitStack() as ctx:
        def sb(name, shape, dt=F32):
            return ctx.enter_context(nc.sbuf_tensor(name, shape, dt))

        def sem(name):
            return ctx.enter_context(nc.semaphore(name))

        w_in = sb("w_in", [P, w_d.shape[1]])
        w_early = w_in[:, 0:CH * 3 * C].rearrange("p (c n) -> p c n", c=CH)
        w_late = w_in[:, CH * 3 * C:CH * 7 * C].rearrange("p (c n) -> p c n", c=CH)
        w_y = w_in[:, CH * 7 * C:]
        IN_U, DT_STATE, GATE = 0, C, C + 2 * NS
        MIX_K, MIX_R, MIX_V, OUT = 0, C, 2 * C, 3 * C
        wmod = sb("wmod", [P, CH, 6 * C])
        w_front = sb("w_front", [P, CH, 2 * NS])
        wf_hi = sb("wf_hi", [P, CH, 2 * NS + C], F32R)
        wf_lo = sb("wf_lo", [P, CH, 2 * NS + C], F32R)
        wl_hi = sb("wl_hi", [P, CH, 3 * C], F32R)
        wl_lo = sb("wl_lo", [P, CH, 3 * C], F32R)
        ident = sb("ident", [P, P])
        cols = sb("cols", [P, 8])
        c_sb = sb("c_sb", [P, CH * NB])
        c_silu = sb("c_silu", [P, CH * NB])
        mod = sb("mod", [P, 12, NB])
        gate_abs = sb("gate_abs", [P, CH, NB])
        gate_sgn = sb("gate_sgn", [P, CH, NB])
        rate = sb("rate", [P, 3])
        half_neg = sb("half_neg", [P, TT])
        eps = sb("eps", [P, TT])
        B_DT, A_LOG, D0, MU_R, MU_K = 0, 1, 2, 4, 6

        x_tok = sb("x_tok", [P, 2, TT, C])
        x_ch = sb("x_ch", [P, 2, CH, T])
        x1 = sb("x1", [P, 2, CH, T])
        stats1 = sb("stats1", [P, TT, 6])
        mv1 = sb("mv1", [P, 5, TT])
        rstd1 = sb("rstd1", [P, TT])
        xn1 = sb("xn1", [P, TT, C])
        stats2 = sb("stats2", [P, TT, 6])
        mv2 = sb("mv2", [P, 5, TT])
        rstd2 = sb("rstd2", [P, TT])
        xn2 = sb("xn2", [P, TT, C])
        h = sb("h", [P, 2, CH, T])
        h_hi = sb("h_hi", [P, CH, T], F32R)
        h_lo = sb("h_lo", [P, CH, T], F32R)
        dt_e = sb("dt_e", [P, T])
        dt_l = sb("dt_l", [P, T])
        decay = sb("decay", [P, T])
        drive = sb("drive", [P, T])
        state = sb("state", [P, T])
        silu = sb("silu", [P, CH, T])
        yg = sb("yg", [P, CH, T])
        z = sb("z", [P, CH, T])
        h2 = sb("h2", [P, CH, T + 1])
        h2_diff = sb("h2_diff", [P, CH, T])
        xr = sb("xr", [P, CH, T])
        xr_hi = sb("xr_hi", [P, CH, T], F32R)
        xr_lo = sb("xr_lo", [P, CH, T], F32R)
        xk = sb("xk", [P, CH, T])
        xk_hi = sb("xk_hi", [P, CH, T], F32R)
        xk_lo = sb("xk_lo", [P, CH, T], F32R)
        k_relu = sb("k_relu", [P, CH, T])
        k_act = sb("k_act", [P, CH, T])
        k_hi = sb("k_hi", [P, CH, T], F32R)
        k_lo = sb("k_lo", [P, CH, T], F32R)
        r_tanh = sb("r_tanh", [P, CH, T])
        r_gate = sb("r_gate", [P, CH, T])
        x2 = sb("x2", [P, CH, T])
        rv = sb("rv", [P, CH, T])

        slot = [ctx.enter_context(nc.psum_tensor(f"slot{i}", [P, CH, T], F32)) for i in range(4)]
        ps_front, ps_y = slot[0], slot[0]
        ps_gate, ps_o = slot[1], slot[1]
        ps_h2, ps_k = slot[2], slot[2]
        ps_x1 = slot[2][:].rearrange("p a b -> p (a b)").rearrange("p (t c) -> p t c", t=TT)
        ps_v, ps_h, ps_r = slot[3], slot[3], slot[3]

        s_wl, s_wy = sem("w_late_in"), sem("w_y_in")
        s_w, s_wmod, s_cols, s_c, s_id = sem("w_in"), sem("wmod_in"), sem("cols_in"), sem("c_in"), sem("ident_in")
        s_xt = [sem("x_tok_in0"), sem("x_tok_in1")]
        s_xc = [sem("x_ch_in0"), sem("x_ch_in1")]
        s_out = [sem("x2_out0"), sem("x2_out1")]
        csilu_ok, mod_ps, mod_ok, front_ps, front_ok = sem("csilu_ok"), sem("mod_ps"), sem("mod_ok"), sem("front_ps"), sem("front_ok")
        mod_step, rate_step, rate_exp, rate_ln, rate_ok = sem("mod_step"), sem("rate_step"), sem("rate_exp"), sem("rate_ln"), sem("rate_ok")
        wl_hi_ok, wl_lo_ok = sem("wl_hi_ok"), sem("wl_lo_ok")
        wsplit_hi, wsplit_lo, consts_ok = sem("wsplit_hi"), sem("wsplit_lo"), sem("consts_ok")
        t1_ps, dt_ps, b_ps, g_ps, y_ps, o_ps = sem("t1_ps"), sem("dt_ps"), sem("b_ps"), sem("g_ps"), sem("y_ps"), sem("o_ps")
        t2_ps, t3_ps, k_ps, r_ps, v_ps = sem("t2_ps"), sem("t3_ps"), sem("k_ps"), sem("r_ps"), sem("v_ps")
        h_ok, hhi_ok, e_ok, l_ok, decay_ok, h2_ok = sem("h_ok"), sem("hhi_ok"), sem("e_ok"), sem("l_ok"), sem("decay_ok"), sem("h2_ok")
        silu_ok, relu_ok, tanh_ok, rgate_ok = sem("silu_ok"), sem("relu_ok"), sem("tanh_ok"), sem("rgate_ok")
        st1_ok, mv1_ok, xn1_ok, st2_ok, mv2_ok, xn2_ok = sem("st1_ok"), sem("mv1_ok"), sem("xn1_ok"), sem("st2_ok"), sem("mv2_ok"), sem("xn2_ok")
        halves1_ok, spread1_ok, halves2_ok, spread2_ok = sem("halves1_ok"), sem("spread1_ok"), sem("halves2_ok"), sem("spread2_ok")
        clip_ok, drive_ok, state_ok, yg_ok, z_ok, x1_ok = sem("clip_ok"), sem("drive_ok"), sem("state_ok"), sem("yg_ok"), sem("z_ok"), sem("x1_ok")
        xk_ok, xr_ok, rv_ok = sem("xk_ok"), sem("xr_ok"), sem("rv_ok")
        xkhi_ok, xklo_ok = sem("xkhi_ok"), sem("xklo_ok")
        xrhi_ok, xrlo_ok, khi_ok, klo_ok = sem("xrhi_ok"), sem("xrlo_ok"), sem("khi_ok"), sem("klo_ok")
        hlo_ok, diff_ok, kact_ok, x2_ok = sem("hlo_ok"), sem("diff_ok"), sem("kact_ok"), sem("x2_ok")
        var1_ok, rstd1_ok, var2_ok, rstd2_ok = sem("var1_ok"), sem("rstd1_ok"), sem("var2_ok"), sem("rstd2_ok")

        def col(j):
            return cols[:, j:j + 1]

        def mod_at(j, k):
            return mod[:, j, bass.ds(k, 1)]

        def number(m, r):
            return 2 * m + r

        def turn(m, r):
            return m + r // 2 + 1

        def schedule(eng, iteration):
            for k in range(3):
                iteration(0, k)
            with eng.Fori(1, NB // 2 - 2) as m:
                for r in (1, 2):
                    iteration(m, r)
            for k in range(NB - 3, NB + 2):
                iteration(0, k)

        def runs(m, r, first, last):
            return not isinstance(m, int) or first <= 2 * m + r <= last

        block = ctx.enter_context(nc.Block())

        @block.sync
        def _(sp):
            sp.dma_start(c_sb[:], c_d).then_inc(s_c, 16)
            sp.dma_start(x_tok[:, 0], x_tok_d[0].rearrange("(t p) c -> p t c", p=P)).then_inc(s_xt[0], 16)
            sp.dma_start(cols[:], cols_d).then_inc(s_cols, 16)
            sp.dma_start(ident[:], ident_d).then_inc(s_id, 16)
            sp.dma_start(w_in[:, 0:CH * 3 * C], w_d[:, 0:CH * 3 * C]).then_inc(s_w, 16)
            sp.dma_start(wmod[:], wmod_d.rearrange("(c p) n -> p c n", p=P)).then_inc(s_wmod, 16)
            sp.dma_start(w_y, w_d[:, CH * 7 * C:]).then_inc(s_wy, 16)
            sp.dma_start(w_in[:, CH * 3 * C:CH * 7 * C], w_d[:, CH * 3 * C:CH * 7 * C]).then_inc(s_wl, 16)
            sp.dma_start(x_tok[:, 1], x_tok_d[1].rearrange("(t p) c -> p t c", p=P)).then_inc(s_xt[1], 16)
            sp.dma_start(x_ch[:, 0], x_ch_d[0].rearrange("(c p) t -> p c t", p=P)).then_inc(s_xc[0], 16)

            def iteration(m, r):
                k = number(m, r)
                if runs(m, r, 0, NB - 3):
                    before(sp, xn1_ok, k + 1)
                    sp.dma_start(x_tok[:, r % 2], x_tok_d[bass.ds(k + 2, 1)].rearrange("b (t p) c -> p (b t) c", p=P)).then_inc(s_xt[r % 2], 16)
                if runs(m, r, 0, NB - 2):
                    q = (r + 1) % 2
                    before(sp, x1_ok, k)
                    sp.dma_start(x_ch[:, q], x_ch_d[bass.ds(k + 1, 1)].rearrange("b (c p) t -> p (b c) t", p=P)).then_inc(s_xc[q], 16)
                if runs(m, r, 2, NB + 1):
                    before(sp, x2_ok, k - 1)
                    sp.dma_start(out_d[bass.ds(k - 2, 1)].rearrange("b (c p) t -> p (b c) t", p=P), x2[:]).then_inc(s_out[r % 2], 16)

            schedule(sp, iteration)
            for q in range(2):
                sp.wait_ge(s_out[q], 16 * (NB // 2))

        @block.tensor
        def _(pe):
            def product(out, w, at, x):
                for d in range(CH):
                    for c in range(CH):
                        last = nc.tensor.matmul(out[:, d, :], w[:, c, at + d * P:at + (d + 1) * P], x[:, c, :],
                                                start=(c == 0), stop=(c == CH - 1))
                return last

            def split_product(outs, w_hi, w_lo, at, x_hi, x_lo, low_there=None, count=0):
                for w, x, first, final in ((w_hi, x_hi, True, False), (w_lo, x_hi, False, False), (w_hi, x_lo, False, True)):
                    if final and low_there is not None:
                        before(pe, low_there, count)
                    for d, out in enumerate(outs):
                        for c in range(CH):
                            last = nc.tensor.matmul(out, w[:, c, at + d * P:at + (d + 1) * P], x[:, c, :],
                                                    start=(first and c == 0), stop=(final and c == CH - 1))
                return last

            pe.wait_ge(s_wmod, 16)
            pe.wait_ge(csilu_ok, 1)
            for j in range(12):
                for c in range(CH):
                    last = nc.tensor.matmul(slot[0][:, 0, j * NB:(j + 1) * NB], wmod[:, c, j * P:(j + 1) * P],
                                            c_silu[:, c * NB:(c + 1) * NB], start=(c == 0), stop=(c == CH - 1))
            last.then_inc(mod_ps, 1)
            pe.wait_ge(s_w, 16)
            for a in range(CH):
                for c in range(CH):
                    last = nc.tensor.matmul(slot[1][:, a, 0:2 * NS], w_early[:, c, IN_U + a * P:IN_U + (a + 1) * P], w_early[:, c, DT_STATE:DT_STATE + 2 * NS],
                                            start=(c == 0), stop=(c == CH - 1))
            last.then_inc(front_ps, 1)
            pe.wait_ge(s_id, 16)

            def to_channels(out, x):
                for c in range(CH):
                    for t in range(TT):
                        last = nc.tensor.transpose(out[:, c, t * P:(t + 1) * P], x[:, t, c * P:(c + 1) * P], ident[:])
                return last

            pe.wait_ge(xn1_ok, 1)
            to_channels(ps_h, xn1).then_inc(t1_ps, 1)

            def iteration(m, r):
                k = number(m, r)
                if runs(m, r, 0, NB - 1):
                    if isinstance(k, int) and k == 0:
                        pe.wait_ge(wsplit_lo, 2)
                        pe.wait_ge(mod_ok, 1)
                    before(pe, hhi_ok, k + 1)
                    before(pe, yg_ok, k)
                    split_product([ps_front[:, 0, :]], wf_hi, wf_lo, 0, h_hi, h_lo, hlo_ok, k + 1).then_inc(dt_ps, 1)
                    split_product([ps_front[:, 1, :]], wf_hi, wf_lo, NS, h_hi, h_lo).then_inc(b_ps, 1)
                    before(pe, x1_ok, k)
                    split_product([ps_gate[:, d, :] for d in range(CH)], wf_hi, wf_lo, 2 * NS, h_hi, h_lo).then_inc(g_ps, 1)
                    if isinstance(k, int) and k == 0:
                        pe.wait_ge(s_wy, 16)
                    before(pe, state_ok, k + 1)
                    for d in range(CH):
                        last = nc.tensor.matmul(ps_y[:, d, :], w_y[:, d * P:(d + 1) * P], state[:], start=True, stop=True)
                    last.then_inc(y_ps, 1)
                if runs(m, r, 1, NB):
                    before(pe, xn2_ok, k)
                    to_channels(ps_h2, xn2).then_inc(t3_ps, 1)
                if runs(m, r, 2, NB + 1):
                    before(pe, khi_ok, k - 1)
                    before(pe, tanh_ok, k - 1)
                    split_product([ps_v[:, d, :] for d in range(CH)], wl_hi, wl_lo, MIX_V, k_hi, k_lo, klo_ok, k - 1).then_inc(v_ps, 1)
                if runs(m, r, 0, NB - 1):
                    if isinstance(k, int) and k == 0:
                        pe.wait_ge(s_wl, 16)
                    before(pe, z_ok, k + 1)
                    before(pe, silu_ok, k + 1)
                    product(ps_o, w_late, OUT, z).then_inc(o_ps, 1)
                if runs(m, r, 0, NB - 2):
                    before(pe, xn1_ok, k + 2)
                    before(pe, hhi_ok, k + 1)
                    before(pe, rv_ok, k - 1)
                    to_channels(ps_h, xn1).then_inc(t1_ps, 1)
                if runs(m, r, 1, NB):
                    if isinstance(k, int) and k == 1:
                        pe.wait_ge(wl_lo_ok, 1)
                    before(pe, xkhi_ok, k)
                    split_product([ps_k[:, d, :] for d in range(CH)], wl_hi, wl_lo, MIX_K, xk_hi, xk_lo, xklo_ok, k).then_inc(k_ps, 1)
                if runs(m, r, 1, NB):
                    before(pe, xrhi_ok, k)
                    before(pe, rv_ok, k - 1)
                    if runs(m, r, 1, NB - 2):
                        before(pe, hhi_ok, k + 2)
                    split_product([ps_r[:, d, :] for d in range(CH)], wl_hi, wl_lo, MIX_R, xr_hi, xr_lo, xrlo_ok, k).then_inc(r_ps, 1)
                if runs(m, r, 0, NB - 1):
                    before(pe, x1_ok, k + 1)
                    before(pe, relu_ok, k)
                    for t in range(TT):
                        for c in range(CH):
                            last = nc.tensor.transpose(ps_x1[:, t, c * P:(c + 1) * P], x1[:, r % 2, c, t * P:(t + 1) * P], ident[:])
                    last.then_inc(t2_ps, 1)

            schedule(pe, iteration)

        @block.scalar
        def _(act):
            act.wait_ge(s_c, 16)
            nc.scalar.activation(c_silu[:], c_sb[:], ACT.Silu).then_inc(csilu_ok, 1)
            nc.scalar.preload_act_table_set("natural_log_exp_and_others")
            act.wait_ge(rate_step, 2)
            nc.scalar.activation(rate[:, 1:2], rate[:, 0:1], ACT.Exp, scale=-1.0).then_inc(rate_exp, 1)
            act.wait_ge(rate_exp, 1)
            nc.scalar.activation(rate[:, 2:3], rate[:, 1:2], ACT.Ln, bias=1.0).then_inc(rate_ln, 1)

            def h_evac(k, q):
                before(act, t1_ps, k + 1)
                before(act, z_ok, k - 1)
                before(act, g_ps, k)
                for c in range(CH):
                    last = nc.scalar.activation(h[:, q, c, :], ps_h[:, c, :], ACT.Identity, bias=mod_at(c, k), scale=mod_at(2 + c, k))
                last.then_inc(h_ok, 1)
                for c in range(CH):
                    last = nc.scalar.activation(h_hi[:, c, :], ps_h[:, c, :], ACT.Identity, bias=mod_at(c, k), scale=mod_at(2 + c, k))
                last.then_inc(hhi_ok, 1)

            act.wait_ge(mod_ok, 1)
            act.wait_ge(rate_ok, 1)
            h_evac(0, 0)
            act.wait_ge(s_wl, 16)
            nc.scalar.copy(wl_hi[:], w_late[:, :, 0:OUT]).then_inc(wl_hi_ok, 1)

            def high_part(hi, x, there, used, done, k):
                before(act, there, k + 1)
                before(act, used, k)
                nc.scalar.copy(hi[:], x[:]).then_inc(done, 1)

            def iteration(m, r):
                k = number(m, r)
                if runs(m, r, 0, NB - 1):
                    nc.scalar.preload_act_table_set("natural_log_exp_and_others")
                    before(act, dt_ps, k + 1)
                    nc.scalar.activation(dt_e[:], ps_front[:, 0, :], ACT.Exp, bias=col(B_DT)).then_inc(e_ok, 1)
                    before(act, clip_ok, k + 1)
                    nc.scalar.activation(dt_l[:], dt_e[:], ACT.Ln, bias=1.0).then_inc(l_ok, 1)
                    before(act, l_ok, k + 1)
                    before(act, state_ok, k)
                    nc.scalar.activation(decay[:], dt_l[:], ACT.Exp, scale=rate[:, 0:1]).then_inc(decay_ok, 1)
                nc.scalar.preload_act_table_set("silu_and_others")
                if runs(m, r, 0, NB - 1):
                    before(act, g_ps, k + 1)
                    before(act, yg_ok, k)
                    nc.scalar.activation(silu[:], ps_gate[:], ACT.Silu).then_inc(silu_ok, 1)
                if runs(m, r, 2, NB + 1):
                    before(act, r_ps, k - 1)
                    nc.scalar.activation(r_tanh[:], ps_r[:], ACT.Tanh, scale=0.5).then_inc(tanh_ok, 1)
                    before(act, tanh_ok, k - 1)
                    before(act, rv_ok, k - 2)
                    for c in range(CH):
                        last = nc.scalar.activation(r_gate[:, c, :], r_tanh[:, c, :], ACT.Identity, bias=mod_at(10 + c, k - 2), scale=mod_at(10 + c, k - 2))
                    last.then_inc(rgate_ok, 1)
                if runs(m, r, 1, NB):
                    before(act, t3_ps, k)
                    before(act, xr_ok, k - 1)
                    for c in range(CH):
                        last = nc.scalar.activation(h2[:, c, 1:T + 1], ps_h2[:, c, :], ACT.Identity, bias=mod_at(6 + c, k - 1), scale=mod_at(8 + c, k - 1))
                    last.then_inc(h2_ok, 1)
                if runs(m, r, 1, NB):
                    high_part(xk_hi, xk, xk_ok, k_ps, xkhi_ok, k - 1)
                    high_part(xr_hi, xr, xr_ok, r_ps, xrhi_ok, k - 1)
                if runs(m, r, 0, NB - 2):
                    h_evac(k + 1, (r + 1) % 2)
                if runs(m, r, 1, NB):
                    before(act, k_ps, k)
                    nc.scalar.activation(k_relu[:], ps_k[:], ACT.Relu).then_inc(relu_ok, 1)
                    before(act, relu_ok, k)
                    before(act, v_ps, k - 1)
                    before(act, klo_ok, k - 1)
                    nc.scalar.activation(k_hi[:], k_relu[:], ACT.Square)
                    nc.scalar.activation(k_act[:], k_relu[:], ACT.Square).then_inc(khi_ok, 1)

            schedule(act, iteration)

        @block.vector
        def _(dve):
            steps = [0]

            def chained(sem_, ins, count=None):
                steps[0] += 1
                ins.then_inc(sem_, 1)
                dve.wait_ge(sem_, steps[0])

            def stats(x, st, mv, st_ok, halves_ok, spread_ok, mv_ok, k):
                for t in range(TT):
                    last = nc.vector.bn_stats(st[:, t, :], x[:, t, :])
                last.then_inc(st_ok, 1)
                before(dve, st_ok, k + 1)
                nc.vector.tensor_tensor(mv[:, 2, :], st[:, :, 1], st[:, :, 4], ALU.subtract)
                nc.vector.tensor_tensor(mv[:, 3, :], st[:, :, 2], st[:, :, 5], ALU.add).then_inc(halves_ok, 1)
                before(dve, halves_ok, k + 1)
                nc.vector.scalar_tensor_tensor(mv[:, 0, :], mv[:, 2, :], -0.5, st[:, :, 1], ALU.mult, ALU.add)
                nc.vector.scalar_tensor_tensor(mv[:, 4, :], mv[:, 2, :], 0.25, mv[:, 2, :], ALU.mult, ALU.mult).then_inc(spread_ok, 1)
                before(dve, spread_ok, k + 1)
                nc.vector.scalar_tensor_tensor(mv[:, 1, :], mv[:, 3, :], 1.0 / C, mv[:, 4, :], ALU.mult, ALU.add).then_inc(mv_ok, 1)

            def normalise(xn, x, mv, rstd, done):
                for t in range(TT):
                    last = nc.vector.tensor_scalar(xn[:, t, :], x[:, t, :], mv[:, 0, t:t + 1], rstd[:, t:t + 1], ALU.subtract, ALU.mult)
                last.then_inc(done, 1)

            def ln1_stats(k, q, n):
                before(dve, s_xt[q], 16 * n)
                stats(x_tok[:, q], stats1, mv1, st1_ok, halves1_ok, spread1_ok, mv1_ok, k)

            def ln1_apply(k, q):
                before(dve, rstd1_ok, k + 1)
                before(dve, t1_ps, k)
                normalise(xn1, x_tok[:, q], mv1, rstd1, xn1_ok)

            nc.vector.memset(half_neg[:], -0.5)
            nc.vector.memset(eps[:], EPS)
            nc.vector.memset(h2[:, :, 0:1], 0.0).then_inc(consts_ok, 1)
            ln1_stats(0, 0, 1)
            dve.wait_ge(s_cols, 16)
            nc.vector.tensor_scalar(rate[:, 1:2], col(A_LOG), -1.0, None, ALU.mult).then_inc(rate_step, 1)
            dve.wait_ge(rate_step, 1)
            nc.vector.tensor_tensor(rate[:, 0:1], rate[:, 1:2], col(A_LOG), ALU.max).then_inc(rate_step, 1)
            ln1_apply(0, 0)
            ln1_stats(1, 1, 1)
            dve.wait_ge(front_ps, 1)
            nc.vector.tensor_copy(w_front[:], slot[1][:, :, 0:2 * NS]).then_inc(front_ok, 1)
            dve.wait_ge(front_ok, 1)
            nc.vector.tensor_copy(wf_hi[:, :, 0:2 * NS], w_front[:])
            nc.vector.tensor_copy(wf_hi[:, :, 2 * NS:], w_early[:, :, GATE:GATE + C]).then_inc(wsplit_hi, 1)
            dve.wait_ge(wsplit_hi, 1)
            nc.vector.tensor_tensor(wf_lo[:, :, 0:2 * NS], w_front[:], wf_hi[:, :, 0:2 * NS].bitcast(F32), ALU.subtract).then_inc(wsplit_lo, 1)
            nc.vector.tensor_tensor(wf_lo[:, :, 2 * NS:], w_early[:, :, GATE:GATE + C], wf_hi[:, :, 2 * NS:].bitcast(F32), ALU.subtract).then_inc(wsplit_lo, 1)
            dve.wait_ge(mod_ps, 1)
            chained(mod_step, nc.vector.tensor_copy(mod[:], slot[0][:, 0, 0:12 * NB].rearrange("p (j b) -> p j b", b=NB)))
            for j in (2, 8):
                chained(mod_step, nc.vector.tensor_scalar(mod[:, j:j + CH, :], mod[:, j:j + CH, :], 1.0, None, ALU.add))
            for j, scale in ((4, 1.0), (10, 0.5)):
                g = mod[:, j:j + CH, :]
                chained(mod_step, nc.vector.tensor_scalar(gate_abs[:], g, -1.0, None, ALU.mult))
                chained(mod_step, nc.vector.tensor_tensor(gate_abs[:], gate_abs[:], g, ALU.max))
                chained(mod_step, nc.vector.tensor_scalar(gate_abs[:], gate_abs[:], GATE_MIN, scale, ALU.max, ALU.mult))
                chained(mod_step, nc.vector.tensor_scalar(gate_sgn[:], g, 0.0, 2.0, ALU.is_ge, ALU.mult))
                chained(mod_step, nc.vector.tensor_scalar(gate_sgn[:], gate_sgn[:], -1.0, None, ALU.add))
                chained(mod_step, nc.vector.tensor_tensor(g, gate_sgn[:], gate_abs[:], ALU.mult))
            dve.wait_ge(rate_ln, 1)
            nc.vector.tensor_scalar(rate[:, 0:1], col(A_LOG), 0.0, RATE_EPS, ALU.max, ALU.add).then_inc(rate_step, 1)
            dve.wait_ge(rate_step, 3)
            nc.vector.tensor_tensor(rate[:, 0:1], rate[:, 0:1], rate[:, 2:3], ALU.add).then_inc(rate_step, 1)
            dve.wait_ge(rate_step, 4)
            nc.vector.tensor_scalar(rate[:, 0:1], rate[:, 0:1], -1.0, None, ALU.mult).then_inc(rate_ok, 1)
            dve.wait_ge(rate_ok, 1)
            nc.vector.tensor_copy(rate[:, 1:2], rate[:, 0:1]).then_inc(mod_ok, 1)

            def low_part(lo, x, hi, there, used, done, k):
                before(dve, there, k + 1)
                before(dve, used, k)
                nc.vector.tensor_tensor(lo[:], x[:], hi[:].bitcast(F32), ALU.subtract).then_inc(done, 1)

            def mix(out, mu, done):
                for c in range(CH):
                    last = nc.vector.scalar_tensor_tensor(out[:, c, :], h2_diff[:, c, :], col(mu + c), h2[:, c, 0:T], ALU.mult, ALU.add)
                last.then_inc(done, 1)

            def iteration(m, r):
                k = number(m, r)
                p = r % 2
                front, middle, tail = runs(m, r, 0, NB - 1), runs(m, r, 1, NB), runs(m, r, 2, NB + 1)
                if middle:
                    before(dve, t2_ps, k)
                    stats(ps_x1, stats2, mv2, st2_ok, halves2_ok, spread2_ok, mv2_ok, k - 1)
                if front:
                    before(dve, e_ok, k + 1)
                    nc.vector.tensor_scalar(dt_e[:], dt_e[:], EXP_MAX, None, ALU.min).then_inc(clip_ok, 1)
                    before(dve, decay_ok, k + 1)
                    before(dve, b_ps, k + 1)
                    nc.vector.scalar_tensor_tensor(drive[:], decay[:], 1.0, ps_front[:, 1, :], ALU.subtract, ALU.mult).then_inc(drive_ok, 1)
                    before(dve, drive_ok, k + 1)
                    before(dve, y_ps, k)
                    nc.vector.tensor_tensor_scan(state[:], decay[:], drive[:], 0.0, ALU.mult, ALU.subtract).then_inc(state_ok, 1)
                if middle:
                    before(dve, rstd2_ok, k)
                    before(dve, t3_ps, k - 1)
                    normalise(xn2, ps_x1, mv2, rstd2, xn2_ok)
                if front:
                    before(dve, y_ps, k + 1)
                    before(dve, silu_ok, k + 1)
                    nc.vector.tensor_tensor(yg[:], silu[:], ps_y[:], ALU.mult).then_inc(yg_ok, 1)
                    before(dve, yg_ok, k + 1)
                    before(dve, o_ps, k)
                    before(dve, h_ok, k + 1)
                    for c in range(CH):
                        last = nc.vector.scalar_tensor_tensor(z[:, c, :], h[:, p, c, :], col(D0 + c), yg[:, c, :], ALU.mult, ALU.add)
                    last.then_inc(z_ok, 1)
                if runs(m, r, 0, NB - 2):
                    ln1_apply(k + 1, (r + 1) % 2)
                if tail:
                    before(dve, v_ps, k - 1)
                    before(dve, rgate_ok, k - 1)
                    before(dve, x2_ok, k - 2)
                    nc.vector.tensor_tensor(rv[:], r_gate[:], ps_v[:], ALU.mult).then_inc(rv_ok, 1)
                if middle:
                    before(dve, diff_ok, k)
                    before(dve, xkhi_ok, k - 1)
                    mix(xk, MU_K, xk_ok)
                if middle:
                    before(dve, xrlo_ok, k - 1)
                    mix(xr, MU_R, xr_ok)
                    low_part(xk_lo, xk, xk_hi, xkhi_ok, k_ps, xklo_ok, k - 1)
                if front:
                    before(dve, o_ps, k + 1)
                    before(dve, s_xc[p], 16 * turn(m, r))
                    before(dve, x2_ok, k - 1)
                    for c in range(CH):
                        last = nc.vector.scalar_tensor_tensor(x1[:, p, c, :], ps_o[:, c, :], mod_at(4 + c, k), x_ch[:, p, c, :], ALU.mult, ALU.add)
                    last.then_inc(x1_ok, 1)
                if runs(m, r, 0, NB - 3):
                    ln1_stats(k + 2, p, turn(m, r + 2))

            schedule(dve, iteration)

        @block.gpsimd
        def _(pool):
            def inv_std(mv, rstd, mv_ok, var_ok, rstd_ok, k):
                before(pool, mv_ok, k + 1)
                nc.gpsimd.tensor_tensor(rstd[:], mv[:, 1, :], eps[:], ALU.add).then_inc(var_ok, 1)
                before(pool, var_ok, k + 1)
                nc.gpsimd.tensor_tensor(rstd[:], rstd[:], half_neg[:], ALU.pow).then_inc(rstd_ok, 1)

            def low_part(lo, x, hi, there, used, done, k):
                before(pool, there, k + 1)
                before(pool, used, k)
                nc.gpsimd.tensor_tensor(lo[:], x, hi[:].bitcast(F32), ALU.subtract).then_inc(done, 1)

            pool.wait_ge(consts_ok, 1)
            inv_std(mv1, rstd1, mv1_ok, var1_ok, rstd1_ok, 0)
            low_part(h_lo, h[:, 0], h_hi, hhi_ok, g_ps, hlo_ok, 0)
            pool.wait_ge(wl_hi_ok, 1)
            nc.gpsimd.tensor_tensor(wl_lo[:], w_late[:, :, 0:OUT], wl_hi[:].bitcast(F32), ALU.subtract).then_inc(wl_lo_ok, 1)

            def iteration(m, r):
                k = number(m, r)
                p = r % 2
                if runs(m, r, 0, NB - 2):
                    inv_std(mv1, rstd1, mv1_ok, var1_ok, rstd1_ok, k + 1)
                if runs(m, r, 1, NB):
                    inv_std(mv2, rstd2, mv2_ok, var2_ok, rstd2_ok, k - 1)
                    before(pool, h2_ok, k)
                    before(pool, xr_ok, k - 1)
                    nc.gpsimd.tensor_tensor(h2_diff[:], h2[:, :, 1:T + 1], h2[:, :, 0:T], ALU.subtract).then_inc(diff_ok, 1)
                if runs(m, r, 2, NB + 1):
                    before(pool, rv_ok, k - 1)
                    before(pool, s_out[(r + 1) % 2], 16 * turn(m, r - 3))
                    nc.gpsimd.tensor_tensor(x2[:], x1[:, p], rv[:], ALU.add).then_inc(x2_ok, 1)
                if runs(m, r, 1, NB):
                    low_part(xr_lo, xr[:], xr_hi, xrhi_ok, r_ps, xrlo_ok, k - 1)
                if runs(m, r, 0, NB - 2):
                    low_part(h_lo, h[:, (r + 1) % 2], h_hi, hhi_ok, g_ps, hlo_ok, k + 1)
                if runs(m, r, 1, NB):
                    low_part(k_lo, k_act[:], k_hi, khi_ok, v_ps, klo_ok, k - 1)

            schedule(pool, iteration)


def kernel(**inputs):
    import concourse.bacc as bacc
    from concourse.bass_utils import run_bass_kernel_spmd

    a = {name.replace("L0_", "").replace("attn_", "").replace("ffn_", ""): np.asarray(v) for name, v in inputs.items()}
    C = a["x"].shape[2]

    def halves(w):
        return w.reshape(-1, P, w.shape[1]).transpose(1, 0, 2).reshape(P, -1)

    x = np.ascontiguousarray(a["x"])
    arrays = {
        "x_tok": x,
        "x_ch": np.ascontiguousarray(x.transpose(0, 2, 1)),
        "weights": np.ascontiguousarray(np.concatenate([
            halves(np.concatenate([a["W_in"][:C], a["W_dt"].T, a["W_state"].T, a["W_in"][C:].T], axis=1)),
            halves(np.concatenate([a["W_k"].T, a["W_r"].T, a["W_v"].T, a["W_out"].T], axis=1)),
            halves(a["W_C"].T),
        ], axis=1)),
        "wmod": np.ascontiguousarray(a["wmod"]),
        "c": np.ascontiguousarray(halves(a["c"].T)),
        "cols": np.ascontiguousarray(np.stack([a["b_dt"], a["A_log"], *(v.reshape(-1, P)[i] for v in (a["D"], a["mu_r"], a["mu_k"])
                                                                        for i in range(2))], axis=1)),
        "ident": np.eye(P, dtype=np.float32),
    }
    arrays = {f"{name}_in": v for name, v in arrays.items()}
    nc = bacc.Bacc("TRN2", target_bir_lowering=False, num_devices=1)
    aps = [nc.dram_tensor(name, v.shape, F32, kind="ExternalInput").ap() for name, v in arrays.items()]
    out = nc.dram_tensor("x2_out", arrays["x_ch_in"].shape, F32, kind="ExternalOutput").ap()
    adaln_block(nc, *aps, out)
    got = run_bass_kernel_spmd(nc, [arrays], core_ids=[0]).results[0]["x2_out"]
    return np.ascontiguousarray(got.transpose(0, 2, 1))
```

```python
from contextlib import ExitStack

import numpy as np

import concourse.bass as bass
from concourse import mybir

F32 = mybir.dt.float32
F32R = mybir.dt.float32r
BF16 = mybir.dt.bfloat16
ALU = mybir.AluOpType
ACT = mybir.ActivationFunctionType

P = 128
EPS = 1e-5
RATE_EPS = 1e-4
DT_MAX = 10.0
GATE_MIN = 0.25


def before(eng, sem, count):
    if not isinstance(count, int) or count > 0:
        eng.wait_ge(sem, count)


def adaln_block(nc, x_tok_d, x_ch_d, w_d, wmod_d, c_d, cols_d, ident_d, out_d):
    NB, T, C = x_tok_d.shape
    CH = C // P
    TT = T // P
    NS = P
    EXP_MAX = float(np.expm1(DT_MAX))

    with ExitStack() as ctx:
        def sb(name, shape, dt=F32):
            return ctx.enter_context(nc.sbuf_tensor(name, shape, dt))

        def sem(name):
            return ctx.enter_context(nc.semaphore(name))

        w_in = sb("w_in", [P, w_d.shape[1]])
        w_early = w_in[:, 0:CH * 3 * C].rearrange("p (c n) -> p c n", c=CH)
        w_late = w_in[:, CH * 3 * C:CH * 7 * C].rearrange("p (c n) -> p c n", c=CH)
        w_y = w_in[:, CH * 7 * C:]
        IN_U, DT_STATE, GATE = 0, C, C + 2 * NS
        MIX_K, MIX_R, MIX_V, OUT = 0, C, 2 * C, 3 * C
        wmod = sb("wmod", [P, CH, 6 * C])
        w_front = sb("w_front", [P, CH, 2 * NS])
        wf_hi = sb("wf_hi", [P, CH, 2 * NS + C], F32R)
        wf_lo = sb("wf_lo", [P, CH, 2 * NS + C], F32R)
        wl_hi = sb("wl_hi", [P, CH, 3 * C], F32R)
        wl_lo = sb("wl_lo", [P, CH, 3 * C], F32R)
        wo_hi = sb("wo_hi", [P, CH, C], F32R)
        wo_lo = sb("wo_lo", [P, CH, C], F32R)
        ident = sb("ident", [P, P])
        cols = sb("cols", [P, 8])
        c_sb = sb("c_sb", [P, CH * NB])
        c_silu = sb("c_silu", [P, CH * NB])
        mod = sb("mod", [P, 12, NB])
        gate_abs = sb("gate_abs", [P, CH, NB])
        gate_sgn = sb("gate_sgn", [P, CH, NB])
        rate = sb("rate", [P, 3])
        half_neg = sb("half_neg", [P, TT])
        eps = sb("eps", [P, TT])
        zeros = sb("zeros", [P, T], BF16)
        B_DT, A_LOG, D0, MU_R, MU_K = 0, 1, 2, 4, 6

        x_tok = sb("x_tok", [P, 2, TT, C])
        x_ch = sb("x_ch", [P, 2, CH, T])
        x1 = sb("x1", [P, 2, CH, T])
        stats1 = sb("stats1", [P, TT, 6])
        mv1 = sb("mv1", [P, 5, TT])
        rstd1 = sb("rstd1", [P, TT])
        shift1 = sb("shift1", [P, TT])
        xn1 = sb("xn1", [P, TT, C])
        stats2 = sb("stats2", [P, TT, 6])
        mv2 = sb("mv2", [P, 5, TT])
        rstd2 = sb("rstd2", [P, TT])
        xn2 = sb("xn2", [P, TT, C])
        h = sb("h", [P, 2, CH, T])
        h_hi = sb("h_hi", [P, CH, T], F32R)
        h_lo = sb("h_lo", [P, CH, T], F32R)
        dt_e = sb("dt_e", [P, T])
        dt_l = sb("dt_l", [P, T])
        decay = sb("decay", [P, T])
        drive = sb("drive", [P, T])
        state = sb("state", [P, T])
        silu = sb("silu", [P, CH, T])
        z = sb("z", [P, CH, T])
        z_hi = sb("z_hi", [P, CH, T], F32R)
        z_lo = sb("z_lo", [P, CH, T], F32R)
        h2 = sb("h2", [P, CH, T + 1])
        h2_diff = sb("h2_diff", [P, CH, T])
        xr = sb("xr", [P, CH, T])
        xr_hi = sb("xr_hi", [P, CH, T], F32R)
        xr_lo = sb("xr_lo", [P, CH, T], F32R)
        xk = sb("xk", [P, CH, T])
        xk_hi = sb("xk_hi", [P, CH, T], F32R)
        xk_lo = sb("xk_lo", [P, CH, T], F32R)
        k_act = sb("k_act", [P, CH, T])
        k_hi = sb("k_hi", [P, CH, T], F32R)
        k_lo = sb("k_lo", [P, CH, T], F32R)
        r_gate = sb("r_gate", [P, CH, T])
        x2 = sb("x2", [P, CH, T])
        rv = sb("rv", [P, CH, T])

        slot = [ctx.enter_context(nc.psum_tensor(f"slot{i}", [P, CH, T], F32)) for i in range(4)]
        ps_front, ps_y, ps_h = slot[0], slot[0], slot[0]
        ps_gate, ps_o = slot[1], slot[1]
        ps_h2, ps_k = slot[2], slot[2]
        ps_x1 = slot[2][:].rearrange("p a b -> p (a b)").rearrange("p (t c) -> p t c", t=TT)
        ps_v, ps_r = slot[3], slot[3]

        s_wl, s_wy = sem("w_late_in"), sem("w_y_in")
        s_w, s_wmod, s_wmod2, s_cols, s_c, s_id = sem("w_in"), sem("wmod_first_in"), sem("wmod_rest_in"), sem("cols_in"), sem("c_in"), sem("ident_in")
        s_xt = [sem("x_tok_in0"), sem("x_tok_in1")]
        s_xc = [sem("x_ch_in0"), sem("x_ch_in1")]
        s_out = [sem("x2_out0"), sem("x2_out1")]
        mod1_ps, mod1_ok = sem("mod1_ps"), sem("mod1_ok")
        csilu_ok, mod_ps, mod_ok, front_ps, front_ok = sem("csilu_ok"), sem("mod_ps"), sem("mod_ok"), sem("front_ps"), sem("front_ok")
        mod_step, rate_step, rate_exp, rate_ln, rate_ok = sem("mod_step"), sem("rate_step"), sem("rate_exp"), sem("rate_ln"), sem("rate_ok")
        wl_hi_ok, wl_lo_ok, wo_hi_ok, wo_lo_ok = sem("wl_hi_ok"), sem("wl_lo_ok"), sem("wo_hi_ok"), sem("wo_lo_ok")
        wsplit_hi, wsplit_lo, consts_ok = sem("wsplit_hi"), sem("wsplit_lo"), sem("consts_ok")
        t1_ps, dt_ps, b_ps, g_ps, y_ps, o_ps = sem("t1_ps"), sem("dt_ps"), sem("b_ps"), sem("g_ps"), sem("y_ps"), sem("o_ps")
        t2_ps, t3_ps, k_ps, r_ps, v_ps = sem("t2_ps"), sem("t3_ps"), sem("k_ps"), sem("r_ps"), sem("v_ps")
        h_ok, hhi_ok, e_ok, l_ok, decay_ok, h2_ok = sem("h_ok"), sem("hhi_ok"), sem("e_ok"), sem("l_ok"), sem("decay_ok"), sem("h2_ok")
        silu_ok, relu_ok, tanh_ok, rgate_ok = sem("silu_ok"), sem("relu_ok"), sem("tanh_ok"), sem("rgate_ok")
        st1_ok, mv1_ok, st2_ok, mv2_ok, xn2_ok = sem("st1_ok"), sem("mv1_ok"), sem("st2_ok"), sem("mv2_ok"), sem("xn2_ok")
        halves1_ok, spread1_ok, halves2_ok, spread2_ok = sem("halves1_ok"), sem("spread1_ok"), sem("halves2_ok"), sem("spread2_ok")
        clip_ok, drive_ok, state_ok, yg_ok, x1_ok = sem("clip_ok"), sem("drive_ok"), sem("state_ok"), sem("yg_ok"), sem("x1_ok")
        xr_ok, rv_ok = sem("xr_ok"), sem("rv_ok")
        xrhi_ok, khi_ok, klo_ok = sem("xrhi_ok"), sem("khi_ok"), sem("klo_ok")
        zeros_ok, shift1_ok = sem("zeros_ok"), sem("shift1_ok")
        var1_ok, rstd1_ok, var2_ok, rstd2_ok = sem("var1_ok"), sem("rstd1_ok"), sem("var2_ok"), sem("rstd2_ok")
        diff_ok = [sem("diff0_ok"), sem("diff1_ok")]
        hlo_ok = [sem("hlo0_ok"), sem("hlo1_ok")]
        z_ok = [sem("z0_ok"), sem("z1_ok")]
        zhi_ok = [sem("zhi0_ok"), sem("zhi1_ok")]
        zlo_ok = [sem("zlo0_ok"), sem("zlo1_ok")]
        xk_ok = [sem("xk0_ok"), sem("xk1_ok")]
        xkhi_ok = [sem("xkhi0_ok"), sem("xkhi1_ok")]
        xklo_ok = [sem("xklo0_ok"), sem("xklo1_ok")]
        xrlo_ok = [sem("xrlo0_ok"), sem("xrlo1_ok")]
        x2_ok = [sem("x2_0_ok"), sem("x2_1_ok")]
        xn1_ok = [sem("xn1_0_ok"), sem("xn1_1_ok")]
        last_xn2_ok, last_h2_ok, last_xk_ok = sem("last_xn2_ok"), sem("last_h2_ok"), sem("last_xk_ok")
        last_v_ps, last_rv_ok, last_x2_ok = sem("last_v_ps"), sem("last_rv_ok"), sem("last_x2_ok")

        def col(j):
            return cols[:, j:j + 1]

        def mod_at(j, k):
            return mod[:, j, bass.ds(k, 1)]

        def number(m, r):
            return 2 * m + r

        def turn(m, r):
            return m + r // 2 + 1

        def schedule(eng, iteration):
            for k in range(3):
                iteration(0, k)
            with eng.Fori(1, NB // 2 - 2) as m:
                for r in (1, 2):
                    iteration(m, r)
            for k in range(NB - 3, NB + 2):
                iteration(0, k)

        def only(m, r, k):
            return isinstance(m, int) and 2 * m + r == k

        def runs(m, r, first, last):
            return not isinstance(m, int) or first <= 2 * m + r <= last

        block = ctx.enter_context(nc.Block())

        @block.sync
        def _(sp):
            sp.dma_start(x_tok[:, 0], x_tok_d[0].rearrange("(t p) c -> p t c", p=P)).then_inc(s_xt[0], 16)
            sp.dma_start(w_in[:, 0:CH * 3 * C], w_d[:, 0:CH * 3 * C]).then_inc(s_w, 16)
            wmod_cols = wmod_d.rearrange("(c p) n -> p c n", p=P)
            sp.dma_start(wmod[:, :, 0:2 * C], wmod_cols[:, :, 0:2 * C]).then_inc(s_wmod, 16)
            sp.dma_start(w_y, w_d[:, CH * 7 * C:]).then_inc(s_wy, 16)
            sp.dma_start(wmod[:, :, 2 * C:], wmod_cols[:, :, 2 * C:]).then_inc(s_wmod2, 16)
            sp.dma_start(x_tok[:, 1], x_tok_d[1].rearrange("(t p) c -> p t c", p=P)).then_inc(s_xt[1], 16)
            sp.dma_start(w_in[:, CH * 3 * C:CH * 7 * C], w_d[:, CH * 3 * C:CH * 7 * C]).then_inc(s_wl, 16)
            sp.dma_start(x_ch[:, 0], x_ch_d[0].rearrange("(c p) t -> p c t", p=P)).then_inc(s_xc[0], 16)

            def iteration(m, r):
                k = number(m, r)
                if runs(m, r, 0, NB - 3):
                    for half_ok in xn1_ok:
                        before(sp, half_ok, k + 1)
                    sp.dma_start(x_tok[:, r % 2], x_tok_d[bass.ds(k + 2, 1)].rearrange("b (t p) c -> p (b t) c", p=P)).then_inc(s_xt[r % 2], 16)
                if runs(m, r, 0, NB - 2):
                    q = (r + 1) % 2
                    before(sp, x1_ok, k)
                    sp.dma_start(x_ch[:, q], x_ch_d[bass.ds(k + 1, 1)].rearrange("b (c p) t -> p (b c) t", p=P)).then_inc(s_xc[q], 16)
                if only(m, r, NB + 1):
                    for c in range(CH):
                        sp.wait_ge(last_x2_ok, c + 1)
                        sp.dma_start(out_d[k - 2, c * P:(c + 1) * P], x2[:, c]).then_inc(s_out[r % 2], 16)
                elif runs(m, r, 2, NB + 1):
                    before(sp, x2_ok[1], k - 1)
                    sp.dma_start(out_d[bass.ds(k - 2, 1)].rearrange("b (c p) t -> p (b c) t", p=P), x2[:]).then_inc(s_out[r % 2], 16)

            schedule(sp, iteration)
            sp.wait_ge(s_out[0], 16 * (NB // 2))
            sp.wait_ge(s_out[1], 16 * (NB // 2 + 1))

        @block.tensor
        def _(pe):
            def passes(outs, w, at, x, halves=range(CH), start=False, stop=False, there=None, count=0):
                for n, c in enumerate(halves):
                    if there is not None:
                        before(pe, there[c], count)
                    for d, out in enumerate(outs):
                        last = nc.tensor.matmul(out, w[:, c, at + d * P:at + (d + 1) * P], x[:, c, :],
                                                start=(start and n == 0), stop=(stop and n == CH - 1))
                return last

            def split_product(outs, w_hi, w_lo, at, x_hi, x_lo, hi_ok=None, lo_ok=None, count=0, lo_halves=range(CH)):
                passes(outs, w_hi, at, x_hi, start=True, there=hi_ok, count=count)
                passes(outs, w_lo, at, x_hi)
                return passes(outs, w_hi, at, x_lo, halves=lo_halves, stop=True, there=lo_ok, count=count)

            def modulation(first, n, out):
                for j in range(n):
                    for c in range(CH):
                        last = nc.tensor.matmul(out[:, j * NB:(j + 1) * NB], wmod[:, c, (first + j) * P:(first + j + 1) * P],
                                                c_silu[:, c * NB:(c + 1) * NB], start=(c == 0), stop=(c == CH - 1))
                return last

            def keep_warm(out, n):
                for _ in range(n):
                    nc.tensor.matmul(out, zeros[:, 0:P], zeros[:], start=True, stop=True)

            pe.wait_ge(zeros_ok, 1)
            keep_warm(slot[0][:, 0, :], 13)
            pe.wait_ge(s_w, 16)
            for a in range(CH):
                for c in range(CH):
                    last = nc.tensor.matmul(slot[1][:, a, 0:2 * NS], w_early[:, c, IN_U + a * P:IN_U + (a + 1) * P], w_early[:, c, DT_STATE:DT_STATE + 2 * NS],
                                            start=(c == 0), stop=(c == CH - 1))
            last.then_inc(front_ps, 1)

            def to_channels(out, x, tiles=range(TT)):
                for c in range(CH):
                    for t in tiles:
                        last = nc.tensor.transpose(out[:, c, t * P:(t + 1) * P], x[:, t, c * P:(c + 1) * P], ident[:])
                return last

            def xn1_to_channels(out, k):
                for half_ok in xn1_ok:
                    before(pe, half_ok, k + 1)
                return to_channels(out, xn1)

            def v_first_part(k):
                before(pe, khi_ok, k - 1)
                before(pe, tanh_ok, k - 1)
                passes([ps_v[:, 0, :]], wl_hi, MIX_V, k_hi, start=True)
                passes([ps_v[:, 0, :]], wl_lo, MIX_V, k_hi)

            def dt_and_b(k):
                before(pe, hhi_ok, k + 1)
                before(pe, yg_ok, k)
                split_product([ps_front[:, 0, :]], wf_hi, wf_lo, 0, h_hi, h_lo, None, hlo_ok, k + 1).then_inc(dt_ps, 1)
                split_product([ps_front[:, 1, :]], wf_hi, wf_lo, NS, h_hi, h_lo).then_inc(b_ps, 1)

            def x1_to_tokens(k, p):
                before(pe, x1_ok, k + 1)
                before(pe, relu_ok, k)
                if isinstance(k, int) and k == 0:
                    pe.wait_ge(mod_ok, 1)
                for t in range(TT):
                    for c in range(CH):
                        last = nc.tensor.transpose(ps_x1[:, t, c * P:(c + 1) * P], x1[:, p, c, t * P:(t + 1) * P], ident[:])
                last.then_inc(t2_ps, 1)

            pe.wait_ge(s_wmod, 16)
            pe.wait_ge(csilu_ok, 1)
            modulation(0, 4, slot[2][:, 0, :]).then_inc(mod1_ps, 1)
            pe.wait_ge(s_id, 16)
            xn1_to_channels(ps_h, 0).then_inc(t1_ps, 1)
            keep_warm(slot[3][:, 0, :], 6)

            def iteration(m, r):
                k = number(m, r)
                if runs(m, r, 0, NB - 1):
                    if only(m, r, 0):
                        pe.wait_ge(wsplit_lo, 1)
                    if not only(m, r, 1):
                        dt_and_b(k)
                    if only(m, r, 0):
                        pe.wait_ge(wsplit_lo, 2)
                    if only(m, r, 1):
                        x1_to_tokens(0, 0)
                    before(pe, x1_ok, k)
                    split_product([ps_gate[:, d, :] for d in range(CH)], wf_hi, wf_lo, 2 * NS, h_hi, h_lo).then_inc(g_ps, 1)
                    if only(m, r, 0):
                        pe.wait_ge(s_wy, 16)
                    if runs(m, r, 2, NB - 1):
                        v_first_part(k)
                    before(pe, state_ok, k + 1)
                    for d in range(CH):
                        last = nc.tensor.matmul(ps_y[:, d, :], w_y[:, d * P:(d + 1) * P], state[:], start=True, stop=True)
                    last.then_inc(y_ps, 1)
                    if only(m, r, 0):
                        xn1_to_channels(slot[3], 1).then_inc(t1_ps, 1)
                        pe.wait_ge(s_wmod2, 16)
                        modulation(4, 8, slot[2][:, 1, :]).then_inc(mod_ps, 1)
                if runs(m, r, 1, NB - 1):
                    before(pe, xn2_ok, k)
                    to_channels(ps_h2, xn2).then_inc(t3_ps, 1)
                if runs(m, r, 2, NB + 1):
                    if only(m, r, NB):
                        v_first_part(k)
                    if only(m, r, NB + 1):
                        before(pe, khi_ok, k - 1)
                        for d in range(CH):
                            for c in range(CH):
                                last = nc.tensor.matmul(slot[0][:, d, :], w_late[:, c, MIX_V + d * P:MIX_V + (d + 1) * P], k_act[:, c, :],
                                                        start=(c == 0), stop=(c == CH - 1))
                            last.then_inc(last_v_ps, 1)
                    else:
                        before(pe, klo_ok, k - 1)
                        passes([ps_v[:, 0, :]], wl_hi, MIX_V, k_lo, stop=True)
                        split_product([ps_v[:, 1, :]], wl_hi, wl_lo, MIX_V + P, k_hi, k_lo).then_inc(v_ps, 1)
                if only(m, r, NB):
                    pe.wait_ge(last_xn2_ok, 1)
                    to_channels(slot[0], xn2, range(TT // 2))
                    before(pe, xn2_ok, k)
                    to_channels(slot[0], xn2, range(TT // 2, TT)).then_inc(t3_ps, 1)
                    keep_warm(slot[1][:, 0, :], 10)
                    for c in range(CH):
                        pe.wait_ge(last_xk_ok, c + 1)
                        for d in range(CH):
                            last = nc.tensor.matmul(ps_k[:, d, :], w_late[:, c, MIX_K + d * P:MIX_K + (d + 1) * P], xk[:, c, :],
                                                    start=(c == 0), stop=(c == CH - 1))
                    last.then_inc(k_ps, 1)
                    before(pe, xrhi_ok, k)
                    before(pe, rv_ok, k - 1)
                    split_product([ps_r[:, d, :] for d in range(CH)], wl_hi, wl_lo, MIX_R, xr_hi, xr_lo, None, xrlo_ok, k).then_inc(r_ps, 1)
                if runs(m, r, 1, NB - 2):
                    before(pe, yg_ok, k + 1)
                    xn1_to_channels(ps_h, k + 1).then_inc(t1_ps, 1)
                if runs(m, r, 0, NB - 1):
                    if only(m, r, 0):
                        dt_and_b(1)
                        pe.wait_ge(wo_lo_ok, 1)
                    if only(m, r, 1):
                        keep_warm(slot[3][:, 0, :], 6)
                    before(pe, silu_ok, k + 1)
                    split_product([ps_o[:, d, :] for d in range(CH)], wo_hi, wo_lo, 0, z_hi, z_lo,
                                  zhi_ok, zlo_ok, k + 1, (1, 0)).then_inc(o_ps, 1)
                if runs(m, r, 1, NB - 1):
                    if only(m, r, 1):
                        pe.wait_ge(wl_lo_ok, 1)
                    split_product([ps_k[:, d, :] for d in range(CH)], wl_hi, wl_lo, MIX_K, xk_hi, xk_lo,
                                  xkhi_ok, xklo_ok, k).then_inc(k_ps, 1)
                    before(pe, xrhi_ok, k)
                    before(pe, rv_ok, k - 1)
                    split_product([ps_r[:, d, :] for d in range(CH)], wl_hi, wl_lo, MIX_R, xr_hi, xr_lo, None, xrlo_ok, k).then_inc(r_ps, 1)
                    x1_to_tokens(k, r % 2)

            schedule(pe, iteration)

        @block.scalar
        def _(act):
            act.dma_start(c_sb[:], c_d).then_inc(s_c, 16)
            act.dma_start(cols[:], cols_d).then_inc(s_cols, 16)
            act.dma_start(ident[:], ident_d).then_inc(s_id, 16)
            act.wait_ge(s_c, 16)
            nc.scalar.activation(c_silu[:], c_sb[:], ACT.Silu).then_inc(csilu_ok, 1)
            nc.scalar.preload_act_table_set("natural_log_exp_and_others")
            act.wait_ge(rate_step, 2)
            nc.scalar.activation(rate[:, 1:2], rate[:, 0:1], ACT.Exp, scale=-1.0).then_inc(rate_exp, 1)
            act.wait_ge(rate_exp, 1)
            nc.scalar.activation(rate[:, 2:3], rate[:, 1:2], ACT.Ln, bias=1.0).then_inc(rate_ln, 1)

            def ln1_apply(k, q):
                before(act, shift1_ok, k + 1)
                before(act, t1_ps, k)
                for t in range(TT // 2):
                    last = nc.scalar.activation(xn1[:, t, :], x_tok[:, q, t, :], ACT.Identity, bias=shift1[:, t:t + 1], scale=rstd1[:, t:t + 1])
                last.then_inc(xn1_ok[0], 1)

            def h_evac(k, q, ps, halves=range(CH)):
                before(act, t1_ps, k + 1)
                before(act, z_ok[1], k - 1)
                for c in halves:
                    last = nc.scalar.activation(h[:, q, c, :], ps[:, c, :], ACT.Identity, bias=mod_at(c, k), scale=mod_at(2 + c, k))
                if c == CH - 1:
                    last.then_inc(h_ok, 1)

            def high_part(hi, x, there, used, done, k):
                before(act, there, k + 1)
                before(act, used, k)
                nc.scalar.copy(hi, x).then_inc(done, 1)

            ln1_apply(0, 0)
            act.wait_ge(mod1_ok, 1)
            h_evac(0, 0, ps_h)
            high_part(h_hi[:], h[:, 0], h_ok, g_ps, hhi_ok, 0)

            def gate_half(k, c):
                before(act, tanh_ok, k + 1)
                return nc.scalar.activation(r_gate[:, c, :], r_gate[:, c, :], ACT.Identity, bias=mod_at(10 + c, k), scale=mod_at(10 + c, k))

            def iteration(m, r):
                k = number(m, r)
                if runs(m, r, 0, NB - 1):
                    nc.scalar.preload_act_table_set("natural_log_exp_and_others")
                    before(act, dt_ps, k + 1)
                    nc.scalar.activation(dt_e[:], ps_front[:, 0, :], ACT.Exp, bias=col(B_DT)).then_inc(e_ok, 1)
                    if runs(m, r, 2, NB - 1):
                        gate_half(k - 2, 0)
                    before(act, clip_ok, k + 1)
                    nc.scalar.activation(dt_l[:], dt_e[:], ACT.Ln, bias=1.0).then_inc(l_ok, 1)
                    before(act, l_ok, k + 1)
                    before(act, state_ok, k)
                    if only(m, r, 0):
                        act.wait_ge(rate_ok, 1)
                    nc.scalar.activation(decay[:], dt_l[:], ACT.Exp, scale=rate[:, 0:1]).then_inc(decay_ok, 1)
                    nc.scalar.preload_act_table_set("silu_and_others")
                    before(act, g_ps, k + 1)
                    before(act, yg_ok, k)
                    nc.scalar.activation(silu[:], ps_gate[:], ACT.Silu).then_inc(silu_ok, 1)
                if runs(m, r, 2, NB + 1):
                    if not runs(m, r, 2, NB - 1):
                        gate_half(k - 2, 0)
                    gate_half(k - 2, 1).then_inc(rgate_ok, 1)
                if runs(m, r, 0, NB - 2):
                    ln1_apply(k + 1, (r + 1) % 2)
                if only(m, r, 0):
                    act.wait_ge(s_wl, 16)
                    nc.scalar.copy(wo_hi[:], w_late[:, :, OUT:]).then_inc(wo_hi_ok, 1)
                if only(m, r, 1):
                    act.wait_ge(mod_ok, 1)
                if runs(m, r, 1, NB):
                    before(act, t3_ps, k)
                    before(act, xr_ok, k - 1)
                    ps = slot[0] if only(m, r, NB) else ps_h2
                    for c in range(CH):
                        last = nc.scalar.activation(h2[:, c, 1:T + 1], ps[:, c, :], ACT.Identity,
                                                    bias=mod_at(6 + c, k - 1), scale=mod_at(8 + c, k - 1))
                        if only(m, r, NB):
                            last.then_inc(last_h2_ok, 1)
                    if not only(m, r, NB):
                        last.then_inc(h2_ok, 1)
                if only(m, r, 0):
                    h_evac(1, 1, slot[3])
                    high_part(h_hi[:], h[:, 1], h_ok, g_ps, hhi_ok, 1)
                if runs(m, r, 0, NB - 1):
                    for c in range(CH):
                        high_part(z_hi[:, c], z[:, c], z_ok[c], o_ps, zhi_ok[c], k)
                for c in range(CH):
                    if runs(m, r, 1, NB - 2):
                        h_evac(k + 1, (r + 1) % 2, ps_h, [c])
                    if runs(m, r, 1, NB - 1):
                        high_part(xk_hi[:, c], xk[:, c], xk_ok[c], k_ps, xkhi_ok[c], k - 1)
                if runs(m, r, 1, NB - 2):
                    high_part(h_hi[:], h[:, (r + 1) % 2], h_ok, g_ps, hhi_ok, k + 1)
                if only(m, r, 0):
                    nc.scalar.copy(wl_hi[:], w_late[:, :, 0:OUT]).then_inc(wl_hi_ok, 1)
                if runs(m, r, 1, NB):
                    high_part(xr_hi[:], xr[:], xr_ok, r_ps, xrhi_ok, k - 1)
                    before(act, k_ps, k)
                    before(act, klo_ok, k - 1)
                    nc.scalar.activation(k_act[:], ps_k[:], ACT.Relu).then_inc(relu_ok, 1)
                    before(act, relu_ok, k)
                    before(act, v_ps, k - 1)
                    if runs(m, r, 1, NB - 1):
                        nc.scalar.activation(k_hi[:], k_act[:], ACT.Square)
                    nc.scalar.activation(k_act[:], k_act[:], ACT.Square).then_inc(khi_ok, 1)
                    before(act, r_ps, k)
                    before(act, rv_ok, k - 1)
                    nc.scalar.activation(r_gate[:], ps_r[:], ACT.Tanh, scale=0.5).then_inc(tanh_ok, 1)

            schedule(act, iteration)

        @block.vector
        def _(dve):
            steps = [0]

            def chained(sem_, ins):
                steps[0] += 1
                ins.then_inc(sem_, 1)
                dve.wait_ge(sem_, steps[0])

            def statistics(x, st, st_ok):
                for t in range(TT):
                    last = nc.vector.bn_stats(st[:, t, :], x[:, t, :])
                last.then_inc(st_ok, 1)

            def mean_variance(st, mv, st_ok, halves_ok, spread_ok, mv_ok, k, negative=False):
                before(dve, st_ok, k + 1)
                nc.vector.tensor_tensor(mv[:, 2, :], st[:, :, 1], st[:, :, 4], ALU.subtract)
                nc.vector.tensor_tensor(mv[:, 3, :], st[:, :, 2], st[:, :, 5], ALU.add).then_inc(halves_ok, 1)
                before(dve, halves_ok, k + 1)
                if negative:
                    nc.vector.scalar_tensor_tensor(mv[:, 0, :], mv[:, 2, :], 0.5, st[:, :, 1], ALU.mult, ALU.subtract)
                else:
                    nc.vector.scalar_tensor_tensor(mv[:, 0, :], mv[:, 2, :], -0.5, st[:, :, 1], ALU.mult, ALU.add)
                nc.vector.scalar_tensor_tensor(mv[:, 4, :], mv[:, 2, :], 0.25, mv[:, 2, :], ALU.mult, ALU.mult).then_inc(spread_ok, 1)
                before(dve, spread_ok, k + 1)
                nc.vector.scalar_tensor_tensor(mv[:, 1, :], mv[:, 3, :], 1.0 / C, mv[:, 4, :], ALU.mult, ALU.add).then_inc(mv_ok, 1)

            def normalise(xn, x, mv, rstd, done, half_done=None):
                for t in range(TT):
                    last = nc.vector.tensor_scalar(xn[:, t, :], x[:, t, :], mv[:, 0, t:t + 1], rstd[:, t:t + 1], ALU.subtract, ALU.mult)
                    if half_done is not None and t == TT // 2 - 1:
                        last.then_inc(half_done, 1)
                last.then_inc(done, 1)

            def ln1_stats(k, q, n):
                before(dve, s_xt[q], 16 * n)
                statistics(x_tok[:, q], stats1, st1_ok)
                before(dve, shift1_ok, k)
                mean_variance(stats1, mv1, st1_ok, halves1_ok, spread1_ok, mv1_ok, k, negative=True)

            def ln1_apply(k, q):
                before(dve, shift1_ok, k + 1)
                before(dve, t1_ps, k)
                for t in range(TT // 2, TT):
                    last = nc.vector.tensor_scalar(xn1[:, t, :], x_tok[:, q, t, :], rstd1[:, t:t + 1], shift1[:, t:t + 1], ALU.mult, ALU.add)
                last.then_inc(xn1_ok[1], 1)

            nc.vector.memset(half_neg[:], -0.5)
            nc.vector.memset(eps[:], EPS)
            nc.vector.memset(h2[:, :, 0:1], 0.0).then_inc(consts_ok, 1)
            ln1_stats(0, 0, 1)
            dve.wait_ge(s_cols, 16)
            nc.vector.tensor_scalar(rate[:, 1:2], col(A_LOG), -1.0, None, ALU.mult).then_inc(rate_step, 1)
            dve.wait_ge(rate_step, 1)
            nc.vector.tensor_tensor(rate[:, 0:1], rate[:, 1:2], col(A_LOG), ALU.max).then_inc(rate_step, 1)
            ln1_apply(0, 0)
            dve.wait_ge(front_ps, 1)
            nc.vector.tensor_copy(w_front[:], slot[1][:, :, 0:2 * NS]).then_inc(front_ok, 1)
            dve.wait_ge(mod1_ps, 1)
            chained(mod_step, nc.vector.tensor_copy(mod[:, 0:4, :], slot[2][:, 0, 0:4 * NB].rearrange("p (j b) -> p j b", b=NB)))
            nc.vector.tensor_scalar(mod[:, 2:4, :], mod[:, 2:4, :], 1.0, None, ALU.add).then_inc(mod1_ok, 1)
            dve.wait_ge(front_ok, 1)
            nc.vector.tensor_copy(wf_hi[:, :, 0:2 * NS], w_front[:])
            nc.vector.tensor_copy(wf_hi[:, :, 2 * NS:], w_early[:, :, GATE:GATE + C]).then_inc(wsplit_hi, 1)
            dve.wait_ge(wsplit_hi, 1)
            nc.vector.tensor_tensor(wf_lo[:, :, 0:2 * NS], w_front[:], wf_hi[:, :, 0:2 * NS].bitcast(F32), ALU.subtract).then_inc(wsplit_lo, 1)
            nc.vector.tensor_tensor(wf_lo[:, :, 2 * NS:], w_early[:, :, GATE:GATE + C], wf_hi[:, :, 2 * NS:].bitcast(F32), ALU.subtract).then_inc(wsplit_lo, 1)
            dve.wait_ge(rate_ln, 1)
            nc.vector.tensor_scalar(rate[:, 0:1], col(A_LOG), 0.0, RATE_EPS, ALU.max, ALU.add).then_inc(rate_step, 1)
            dve.wait_ge(rate_step, 3)
            nc.vector.tensor_tensor(rate[:, 0:1], rate[:, 0:1], rate[:, 2:3], ALU.add).then_inc(rate_step, 1)
            dve.wait_ge(rate_step, 4)
            nc.vector.tensor_scalar(rate[:, 0:1], rate[:, 0:1], -1.0, None, ALU.mult).then_inc(rate_ok, 1)
            dve.wait_ge(hhi_ok, 1)
            for c in range(CH):
                nc.vector.tensor_tensor(h_lo[:, c], h[:, 0, c], h_hi[:, c].bitcast(F32), ALU.subtract).then_inc(hlo_ok[c], 1)
            ln1_stats(1, 1, 1)

            def rest_of_modulation():
                dve.wait_ge(mod_ps, 1)
                chained(mod_step, nc.vector.tensor_copy(mod[:, 4:12, :], slot[2][:, 1, 0:8 * NB].rearrange("p (j b) -> p j b", b=NB)))
                chained(mod_step, nc.vector.tensor_scalar(mod[:, 8:10, :], mod[:, 8:10, :], 1.0, None, ALU.add))
                for j, scale in ((4, 1.0), (10, 0.5)):
                    g = mod[:, j:j + CH, :]
                    chained(mod_step, nc.vector.tensor_scalar(gate_abs[:], g, -1.0, None, ALU.mult))
                    chained(mod_step, nc.vector.tensor_tensor(gate_abs[:], gate_abs[:], g, ALU.max))
                    chained(mod_step, nc.vector.tensor_scalar(gate_abs[:], gate_abs[:], GATE_MIN, scale, ALU.max, ALU.mult))
                    chained(mod_step, nc.vector.tensor_scalar(gate_sgn[:], g, 0.0, 2.0, ALU.is_ge, ALU.mult))
                    chained(mod_step, nc.vector.tensor_scalar(gate_sgn[:], gate_sgn[:], -1.0, None, ALU.add))
                    chained(mod_step, nc.vector.tensor_tensor(g, gate_sgn[:], gate_abs[:], ALU.mult))
                nc.vector.sem_inc(mod_ok, 1)

            def low_part(lo, x, hi, there, used, done, k):
                before(dve, there, k + 1)
                before(dve, used, k)
                nc.vector.tensor_tensor(lo, x, hi.bitcast(F32), ALU.subtract).then_inc(done, 1)

            def clip_dt(k):
                before(dve, e_ok, k + 1)
                nc.vector.tensor_scalar(dt_e[:], dt_e[:], EXP_MAX, None, ALU.min).then_inc(clip_ok, 1)

            def scan(k):
                before(dve, decay_ok, k + 1)
                before(dve, b_ps, k + 1)
                nc.vector.scalar_tensor_tensor(drive[:], decay[:], 1.0, ps_front[:, 1, :], ALU.subtract, ALU.mult).then_inc(drive_ok, 1)
                before(dve, drive_ok, k + 1)
                before(dve, y_ps, k)
                nc.vector.tensor_tensor_scan(state[:], decay[:], drive[:], 0.0, ALU.mult, ALU.subtract).then_inc(state_ok, 1)

            def difference(c, done):
                nc.vector.tensor_tensor(h2_diff[:, c], h2[:, c, 1:T + 1], h2[:, c, 0:T], ALU.subtract).then_inc(done, 1)

            def z_low_part(k):
                low_part(z_lo[:, 1], z[:, 1], z_hi[:, 1], zhi_ok[1], o_ps, zlo_ok[1], k)

            def gated_v(k):
                before(dve, v_ps, k - 1)
                before(dve, rgate_ok, k - 1)
                nc.vector.tensor_tensor(rv[:], r_gate[:], ps_v[:], ALU.mult).then_inc(rv_ok, 1)

            def second_residual(m, r):
                k = number(m, r)
                before(dve, rv_ok, k - 1)
                before(dve, s_out[(r + 1) % 2], 16 * turn(m, r - 3))
                for c in range(CH):
                    nc.vector.tensor_tensor(x2[:, c], x1[:, r % 2, c], rv[:, c], ALU.add).then_inc(x2_ok[c], 1)

            def mix(out, mu, c):
                return nc.vector.scalar_tensor_tensor(out[:, c, :], h2_diff[:, c, :], col(mu + c), h2[:, c, 0:T], ALU.mult, ALU.add)

            def iteration(m, r):
                k = number(m, r)
                p = r % 2
                front, middle, tail = runs(m, r, 0, NB - 1), runs(m, r, 1, NB), runs(m, r, 2, NB + 1)
                if middle:
                    before(dve, t2_ps, k)
                    statistics(ps_x1, stats2, st2_ok)
                if front and not only(m, r, 1):
                    clip_dt(k)
                if middle:
                    mean_variance(stats2, mv2, st2_ok, halves2_ok, spread2_ok, mv2_ok, k - 1)
                if runs(m, r, 1, NB - 2):
                    ln1_apply(k + 1, (r + 1) % 2)
                if front and not only(m, r, 1):
                    scan(k)
                if only(m, r, 0):
                    ln1_apply(1, 1)
                if middle:
                    before(dve, rstd2_ok, k)
                    before(dve, t3_ps, k - 1)
                    normalise(xn2, ps_x1, mv2, rstd2, xn2_ok, last_xn2_ok if only(m, r, NB) else None)
                if front:
                    before(dve, y_ps, k + 1)
                    before(dve, silu_ok, k + 1)
                    nc.vector.tensor_tensor(silu[:], silu[:], ps_y[:], ALU.mult).then_inc(yg_ok, 1)
                    before(dve, yg_ok, k + 1)
                    before(dve, zhi_ok[1], k)
                    before(dve, zlo_ok[0], k)
                    before(dve, h_ok, k + 1)
                    for c in range(CH):
                        nc.vector.scalar_tensor_tensor(z[:, c, :], h[:, p, c, :], col(D0 + c), silu[:, c, :], ALU.mult, ALU.add).then_inc(z_ok[c], 1)
                if only(m, r, 0):
                    dve.wait_ge(wo_hi_ok, 1)
                    nc.vector.tensor_tensor(wo_lo[:], w_late[:, :, OUT:], wo_hi[:].bitcast(F32), ALU.subtract).then_inc(wo_lo_ok, 1)
                    ln1_stats(2, 0, 2)
                if front and not middle:
                    z_low_part(k)
                if only(m, r, 0):
                    rest_of_modulation()
                if only(m, r, NB + 1):
                    before(dve, rgate_ok, k - 1)
                    before(dve, s_out[(r + 1) % 2], 16 * turn(m, r - 3))
                    for c in range(CH):
                        dve.wait_ge(last_v_ps, c + 1)
                        nc.vector.tensor_tensor(rv[:, c], r_gate[:, c], slot[0][:, c], ALU.mult).then_inc(last_rv_ok, 1)
                        dve.wait_ge(last_rv_ok, c + 1)
                        nc.vector.tensor_tensor(x2[:, c], x1[:, p, c], rv[:, c], ALU.add).then_inc(last_x2_ok, 1)
                if only(m, r, NB):
                    gated_v(k)
                    for c in range(CH):
                        dve.wait_ge(last_h2_ok, c + 1)
                        difference(c, diff_ok[0])
                        before(dve, diff_ok[0], k + c)
                        mix(xk, MU_K, c).then_inc(last_xk_ok, 1)
                    mix(xr, MU_R, 0)
                    mix(xr, MU_R, 1).then_inc(xr_ok, 1)
                    second_residual(m, r)
                    for c in range(CH):
                        low_part(xr_lo[:, c], xr[:, c], xr_hi[:, c], xrhi_ok, r_ps, xrlo_ok[c], k - 1)
                elif middle:
                    before(dve, h2_ok, k)
                    difference(0, diff_ok[0])
                    before(dve, diff_ok[0], k)
                    before(dve, xkhi_ok[1], k - 1)
                    before(dve, xklo_ok[1], k - 1)
                    mix(xk, MU_K, 0).then_inc(xk_ok[0], 1)
                    z_low_part(k)
                    before(dve, diff_ok[1], k)
                    mix(xk, MU_K, 1).then_inc(xk_ok[1], 1)
                    before(dve, xrhi_ok, k - 1)
                    before(dve, xrlo_ok[1], k - 1)
                    mix(xr, MU_R, 0)
                    mix(xr, MU_R, 1).then_inc(xr_ok, 1)
                    if tail:
                        gated_v(k)
                        second_residual(m, r)
                if only(m, r, 0):
                    clip_dt(1)
                    scan(1)
                if front:
                    before(dve, o_ps, k + 1)
                    before(dve, s_xc[p], 16 * turn(m, r))
                    for c in range(CH):
                        before(dve, x2_ok[c], k - 1)
                        last = nc.vector.scalar_tensor_tensor(x1[:, p, c, :], ps_o[:, c, :], mod_at(4 + c, k), x_ch[:, p, c, :], ALU.mult, ALU.add)
                    last.then_inc(x1_ok, 1)
                if runs(m, r, 1, NB - 3):
                    ln1_stats(k + 2, p, turn(m, r + 2))

            schedule(dve, iteration)

        @block.gpsimd
        def _(pool):
            def inv_std(mv, rstd, mv_ok, var_ok, rstd_ok, k):
                before(pool, mv_ok, k + 1)
                nc.gpsimd.tensor_tensor(rstd[:], mv[:, 1, :], eps[:], ALU.add).then_inc(var_ok, 1)
                before(pool, var_ok, k + 1)
                nc.gpsimd.tensor_tensor(rstd[:], rstd[:], half_neg[:], ALU.pow).then_inc(rstd_ok, 1)

            def low_part(lo, x, hi, there, used, done, k):
                before(pool, there, k + 1)
                before(pool, used, k)
                nc.gpsimd.tensor_tensor(lo, x, hi.bitcast(F32), ALU.subtract).then_inc(done, 1)

            def h_low_parts(k, q):
                for c in range(CH):
                    low_part(h_lo[:, c], h[:, q, c], h_hi[:, c], hhi_ok, g_ps, hlo_ok[c], k)

            def ln1_scale(k):
                for half_ok in xn1_ok:
                    before(pool, half_ok, k)
                inv_std(mv1, rstd1, mv1_ok, var1_ok, rstd1_ok, k)
                before(pool, rstd1_ok, k + 1)
                nc.gpsimd.tensor_tensor(shift1[:], mv1[:, 0, :], rstd1[:], ALU.mult).then_inc(shift1_ok, 1)

            nc.gpsimd.memset(zeros[:], 0.0).then_inc(zeros_ok, 1)
            pool.wait_ge(consts_ok, 1)
            ln1_scale(0)

            def iteration(m, r):
                k = number(m, r)
                if runs(m, r, 0, NB - 2) and not only(m, r, 1):
                    ln1_scale(k + 1)
                if only(m, r, NB):
                    low_part(k_lo[:], k_act[:], k_hi[:], khi_ok, v_ps, klo_ok, k - 2)
                if runs(m, r, 1, NB):
                    inv_std(mv2, rstd2, mv2_ok, var2_ok, rstd2_ok, k - 1)
                if runs(m, r, 2, NB - 1):
                    low_part(k_lo[:], k_act[:], k_hi[:], khi_ok, v_ps, klo_ok, k - 2)
                if runs(m, r, 1, NB - 1):
                    before(pool, h2_ok, k)
                    before(pool, xr_ok, k - 1)
                    nc.gpsimd.tensor_tensor(h2_diff[:, 1], h2[:, 1, 1:T + 1], h2[:, 1, 0:T], ALU.subtract).then_inc(diff_ok[1], 1)
                if only(m, r, 0):
                    h_low_parts(1, 1)
                if runs(m, r, 0, NB - 1):
                    low_part(z_lo[:, 0], z[:, 0], z_hi[:, 0], zhi_ok[0], o_ps, zlo_ok[0], k)
                if runs(m, r, 1, NB - 1):
                    for c in range(CH):
                        low_part(xk_lo[:, c], xk[:, c], xk_hi[:, c], xkhi_ok[c], k_ps, xklo_ok[c], k - 1)
                    for c in range(CH):
                        low_part(xr_lo[:, c], xr[:, c], xr_hi[:, c], xrhi_ok, r_ps, xrlo_ok[c], k - 1)
                if runs(m, r, 1, NB - 2):
                    h_low_parts(k + 1, (r + 1) % 2)
                if only(m, r, 0):
                    ln1_scale(2)
                    pool.wait_ge(wl_hi_ok, 1)
                    nc.gpsimd.tensor_tensor(wl_lo[:], w_late[:, :, 0:OUT], wl_hi[:].bitcast(F32), ALU.subtract).then_inc(wl_lo_ok, 1)

            schedule(pool, iteration)


def kernel(**inputs):
    import concourse.bacc as bacc
    from concourse.bass_utils import run_bass_kernel_spmd

    a = {name.replace("L0_", "").replace("attn_", "").replace("ffn_", ""): np.asarray(v) for name, v in inputs.items()}
    C = a["x"].shape[2]

    def halves(w):
        return w.reshape(-1, P, w.shape[1]).transpose(1, 0, 2).reshape(P, -1)

    x = np.ascontiguousarray(a["x"])
    arrays = {
        "x_tok": x,
        "x_ch": np.ascontiguousarray(x.transpose(0, 2, 1)),
        "weights": np.ascontiguousarray(np.concatenate([
            halves(np.concatenate([a["W_in"][:C], a["W_dt"].T, a["W_state"].T, a["W_in"][C:].T], axis=1)),
            halves(np.concatenate([a["W_k"].T, a["W_r"].T, a["W_v"].T, a["W_out"].T], axis=1)),
            halves(a["W_C"].T),
        ], axis=1)),
        "wmod": np.ascontiguousarray(a["wmod"]),
        "c": np.ascontiguousarray(halves(a["c"].T)),
        "cols": np.ascontiguousarray(np.stack([a["b_dt"], a["A_log"], *(v.reshape(-1, P)[i] for v in (a["D"], a["mu_r"], a["mu_k"])
                                                                        for i in range(2))], axis=1)),
        "ident": np.eye(P, dtype=np.float32),
    }
    arrays = {f"{name}_in": v for name, v in arrays.items()}
    nc = bacc.Bacc("TRN2", target_bir_lowering=False, num_devices=1)
    aps = [nc.dram_tensor(name, v.shape, F32, kind="ExternalInput").ap() for name, v in arrays.items()]
    out = nc.dram_tensor("x2_out", arrays["x_ch_in"].shape, F32, kind="ExternalOutput").ap()
    adaln_block(nc, *aps, out)
    got = run_bass_kernel_spmd(nc, [arrays], core_ids=[0]).results[0]["x2_out"]
    return np.ascontiguousarray(got.transpose(0, 2, 1))
```
